# Optimizing a Trainium2 kernel written in Bass

```python
import numpy as np
import jax
import jax.numpy as jnp

def _softmax(x, axis=-1):
    return jax.nn.softmax(x, axis=axis)

def _gelu(x):
    return jax.nn.gelu(x, approximate=True)

def _silu(x):
    return jax.nn.silu(x)

def _sigmoid(x):
    return jax.nn.sigmoid(x)

def _layernorm(x, axis=-1, eps=1e-05):
    m = jnp.mean(x, axis=axis, keepdims=True)
    v = jnp.var(x, axis=axis, keepdims=True)
    return (x - m) / jnp.sqrt(v + eps)

def _scatter_add(tgt, idx, src, axis=0):
    return tgt.at[idx].add(src)

def _segment_sum(src, seg, n):
    return jax.ops.segment_sum(src, seg, n)
kernel_name = 'mk_gnn_ffn_d1_gnn_r8_060b37'

def setup_inputs(seed: int=0):
    np.random.seed(seed)
    _w = jnp.asarray

    def _rec_inputs():
        import jax
        import jax.numpy as jnp
        _gk = jax.random.key(seed)
        x = -0.0002117 + 1 * jax.random.normal(jax.random.fold_in(_gk, 1), (12500, 256), jnp.float32)
        _s = jax.random.randint(jax.random.fold_in(_gk, 2), (100000,), 0, 12500, jnp.int32)
        _d = jax.random.randint(jax.random.fold_in(_gk, 3), (100000,), 0, 12500, jnp.int32)
        _loop = jnp.arange(12500, dtype=jnp.int32)
        src = jnp.concatenate([_s, _d, _loop])
        dst = jnp.concatenate([_d, _s, _loop])
        _o = jnp.argsort(dst, stable=True)
        src = src[_o]
        dst = dst[_o]
        edge_weight = jax.random.uniform(jax.random.fold_in(_gk, 12), (212500,), jnp.float32, 0.0, 1)
        return (x, src, dst, edge_weight)
    x, src, dst, edge_weight = _rec_inputs()

    def _L0_gnn_setup():
        import jax, jax.numpy as jnp
        import numpy as np
        N_NODES = 12500
        N_EDGES = 400000
        IN_C = 256
        OUT_C = 256
        key = jax.random.key(seed)
        k1, k2, k3, k4, k5 = jax.random.split(key, 5)
        limit = float(np.sqrt(6.0 / (IN_C + OUT_C)))
        W = jax.random.uniform(k2, (IN_C, OUT_C), jnp.float32, -limit, limit)
        return {'x': jax.random.normal(k1, (N_NODES, IN_C), jnp.float32), 'W': W, 'bias': jnp.zeros((OUT_C,), jnp.float32), 'edge_row': jax.random.randint(k3, (N_EDGES,), 0, N_NODES, jnp.int32), 'edge_col': jax.random.randint(k4, (N_EDGES,), 0, N_NODES, jnp.int32), 'edge_val': jax.random.uniform(k5, (N_EDGES,), jnp.float32)}
    _L0_gnn_all = _L0_gnn_setup()
    _L0_gnn_in = {k: v for k, v in _L0_gnn_all.items() if k in ('W', 'bias')}
    del _L0_gnn_all

    def _L0_ffn_setup():
        import jax, jax.numpy as jnp
        import numpy as np
        E = 8
        K = 2
        D = 256
        H = 512
        DOUT = 256
        EPS = 1e-05
        key = jax.random.key(seed)
        ks = jax.random.split(key, 9)
        s = 0.02
        return {'x': jax.random.normal(ks[0], (4, 1024, D), jnp.float32), 'gamma': 1.0 + 0.05 * jax.random.normal(ks[1], (D,), jnp.float32), 'beta': 0.05 * jax.random.normal(ks[2], (D,), jnp.float32), 'Wr': 0.01 * jax.random.normal(ks[3], (D, E), jnp.float32), 'br': jnp.zeros((E,), jnp.float32), 'W1': s * jax.random.normal(ks[4], (E, D, H), jnp.float32), 'b1': s * jax.random.normal(ks[5], (E, H), jnp.float32), 'W2': s * jax.random.normal(ks[6], (E, H, DOUT), jnp.float32), 'b2': s * jax.random.normal(ks[7], (E, DOUT), jnp.float32)}
    _L0_ffn_all = _L0_ffn_setup()
    _L0_ffn_in = {k: v for k, v in _L0_ffn_all.items() if k in ('gamma', 'beta', 'Wr', 'br', 'W1', 'b1', 'W2', 'b2')}
    del _L0_ffn_all
    return {'x': x, 'src': src, 'dst': dst, 'edge_weight': edge_weight, 'L0_gnn_W': _L0_gnn_in['W'], 'L0_gnn_bias': _L0_gnn_in['bias'], 'L0_ffn_gamma': _L0_ffn_in['gamma'], 'L0_ffn_beta': _L0_ffn_in['beta'], 'L0_ffn_Wr': _L0_ffn_in['Wr'], 'L0_ffn_br': _L0_ffn_in['br'], 'L0_ffn_W1': _L0_ffn_in['W1'], 'L0_ffn_b1': _L0_ffn_in['b1'], 'L0_ffn_W2': _L0_ffn_in['W2'], 'L0_ffn_b2': _L0_ffn_in['b2']}

def reference(x, src, dst, edge_weight, L0_gnn_W, L0_gnn_bias, L0_ffn_gamma, L0_ffn_beta, L0_ffn_Wr, L0_ffn_br, L0_ffn_W1, L0_ffn_b1, L0_ffn_W2, L0_ffn_b2):
    import jax
    import jax.numpy as jnp

    def _L0_gnn_ref(x, W, bias, edge_row, edge_col, edge_val):
        import jax, jax.numpy as jnp
        import numpy as np
        N_NODES = 12500
        N_EDGES = 400000
        IN_C = 256
        OUT_C = 256
        h = x @ W
        msgs = h[edge_col] * edge_val[:, None]
        agg = jax.ops.segment_sum(msgs, edge_row, num_segments=N_NODES)
        return agg + bias

    def _L0_ffn_ref(x, gamma, beta, Wr, br, W1, b1, W2, b2):
        import jax, jax.numpy as jnp
        import numpy as np
        E = 8
        K = 2
        D = 256
        H = 512
        DOUT = 256
        EPS = 1e-05
        mu = jnp.mean(x, axis=-1, keepdims=True)
        var = jnp.mean(jnp.square(x - mu), axis=-1, keepdims=True)
        xn = (x - mu) * jax.lax.rsqrt(var + EPS) * gamma + beta
        logits = jnp.einsum('bsd,de->bse', xn, Wr) + br
        top_vals, top_idx = jax.lax.top_k(logits, K)
        w = jax.nn.softmax(top_vals, axis=-1)
        w_full = jnp.einsum('bsk,bske->bse', w, jax.nn.one_hot(top_idx, E, dtype=w.dtype))
        y = jnp.zeros(x.shape[:-1] + (DOUT,), x.dtype)
        for e in range(E):
            h = jax.nn.gelu(jnp.einsum('bsd,dh->bsh', xn, W1[e]) + b1[e], approximate=False)
            y_e = jnp.einsum('bsh,hd->bsd', h, W2[e]) + b2[e]
            y = y + y_e * w_full[..., e, None]
        return y
    x = x + _L0_gnn_ref(_layernorm(x, axis=-1), L0_gnn_W, L0_gnn_bias, src, dst, edge_weight)
    x = x + _L0_ffn_ref(_layernorm(x, axis=-1)[None], L0_ffn_gamma, L0_ffn_beta, L0_ffn_Wr, L0_ffn_br, L0_ffn_W1, L0_ffn_b1, L0_ffn_W2, L0_ffn_b2)[0]
    return x

_drawn_inputs = setup_inputs


def setup_inputs(seed=0):
    import zlib

    import numpy as np

    out = dict(_drawn_inputs(seed))
    spreads = {'L0_gnn_bias': (0.0, 0.1), 'L0_ffn_br': (0.0, 0.373)}
    factors = {'L0_ffn_gamma': 8.0,
     'L0_ffn_beta': 8.0,
     'L0_ffn_Wr': 3.777,
     'L0_ffn_W1': 2.729,
     'L0_ffn_b1': 31.643,
     'L0_ffn_b2': 8.0}
    for name, (base, spread) in spreads.items():
        noise = np.random.default_rng([zlib.crc32(name.encode()), seed]).standard_normal(out[name].shape)
        drawn = base * np.exp(spread * noise) if base else spread * noise
        out[name] = jnp.asarray(drawn.astype(out[name].dtype))
    for name, factor in factors.items():
        out[name] = (out[name] * factor).astype(out[name].dtype)
    return out
```

```python
import concourse.bass as bass
from concourse import mybir
from contextlib import ExitStack


def gnn_moe_layer_kernel(
    nc: bass.Bass,
    x: bass.AP,
    src: bass.AP,
    dst: bass.AP,
    edge_weight: bass.AP,
    gnn_W: bass.AP,
    gnn_bias: bass.AP,
    gamma: bass.AP,
    beta: bass.AP,
    Wr: bass.AP,
    br: bass.AP,
    W1: bass.AP,
    b1: bass.AP,
    W2: bass.AP,
    b2: bass.AP,
    h_table: bass.AP,
    edge_list: bass.AP,
    out: bass.AP,
):
    fp32 = mybir.dt.float32
    fp16 = mybir.dt.float16
    bf16 = mybir.dt.bfloat16
    i32 = mybir.dt.int32
    u32 = mybir.dt.uint32
    ALU = mybir.AluOpType
    ACT = mybir.ActivationFunctionType
    AX = mybir.AxisListType
    ds = bass.ds

    P = 128
    N, D = x.shape
    E = src.shape[0]
    NE, _, HID = W1.shape
    KD = D // P
    KH = HID // P
    NT = -(-N // P)
    PAD = NT * P - N
    EPS = 1e-5
    WSCALE = 64.0

    GC = 4
    NG = 4
    TC = GC * NG
    COLS = E // P
    LEFT = E - COLS * P
    TURNS = -(-(COLS + (LEFT > 0)) // TC)
    CH = TURNS * TC
    NB = NT + 2
    assert NB * GC <= 512 and NT < TURNS and PAD > 0

    BLK = 32
    SEG = 8
    RECB = 4
    MAXCH = COLS + 1 + NT
    SLOTS = 32
    assert BLK == SLOTS and MAXCH < 2048

    SB = 4
    NSB = (NT - 2) // SB
    assert NT == 2 + SB * NSB and NSB % 2 == 0
    NHC = NE * KH
    YPS = SB * NE + SB

    ctx = ExitStack()
    with ctx:
        ctx.enter_context(nc.allow_non_contiguous_dma(reason="small constants, one element per row"))

        def sb(name, shape, dt):
            return ctx.enter_context(nc.sbuf_tensor(name, shape, dt))

        def sem(name):
            return ctx.enter_context(nc.semaphore(name))

        chosen = sb("chosen", [P, GC, NB], fp32)
        pos_f = sb("pos_f", [P, TC], fp32)
        pos_i = sb("pos_i", [P, TC], i32)
        pos_a = sb("pos_a", [P, TC], i32)
        pos_b = sb("pos_b", [P, TC], i32)
        pos_c = sb("pos_c", [P, TC], i32)
        list_row = [sb(f"list_row{g}", [P, GC], i32) for g in range(NG)]
        record = [sb(f"record{g}", [P, GC, 4], fp32) for g in range(NG)]

        cnt_f = sb("cnt_f", [P, NB], fp32)
        cnt_i = sb("cnt_i", [P, NB], i32)
        nch_i = sb("nch_i", [P, NB], i32)
        nch_f = sb("nch_f", [P, NB], fp32)
        ones_f = sb("ones_f", [P, P], fp32)
        start_f = sb("start_f", [P, NB + 1], fp32)
        start_i = sb("start_i", [P, NB + 1], i32)
        run_row = sb("run_row", [1, 1, NB], fp32)
        blocks_f = sb("blocks_f", [P, 1], fp32)
        blocks_i = sb("blocks_i", [P, 1], i32)
        blocks_n = sb("blocks_n", [P, 1], i32)

        ident = sb("ident", [P, P], fp32)
        iota_i = sb("iota_i", [P, P], i32)
        iota_h = sb("iota_h", [P, P], fp16)
        iota_b = sb("iota_b", [P, NB], bf16)
        ones_b = sb("ones_b", [P, P], bf16)
        before_b = sb("before_b", [P, P], bf16)
        zero_h = sb("zero_h", [1, 512], fp16)
        one_h = sb("one_h", [1, P], fp16)
        bias_f = sb("bias_f", [1, D], fp32)
        bias_hl = sb("bias_hl", [1, 2 * D], fp16)
        gam = sb("gam", [P, KD], fp32)
        bet = sb("bet", [P, KD], fp32)
        b1_t = sb("b1_t", [P, NHC], fp32)
        wr_t = sb("wr_t", [P, KD, NE], fp32)
        br_t = sb("br_t", [1, NE], fp32)
        b2_t = sb("b2_t", [P, SB, D], fp32)
        w_t = sb("w_t", [P, KD, D], fp32)
        w1h = sb("w1h", [P, NE, KD, HID], fp16)
        w1l = sb("w1l", [P, NE, KD, HID], fp16)
        w2h = sb("w2h", [P, NE, KH, D], fp16)
        w2l = sb("w2l", [P, NE, KH, D], fp16)

        xt = [sb(f"xt{i}", [P, D], fp32) for i in range(2)]
        z1 = sb("z1", [P, D], fp32)
        stats = sb("stats", [P, 6], fp32)
        mv = sb("mv", [P, 2], fp32)
        ve = sb("ve", [P, 1], fp32)
        vh = sb("vh", [P, 1], fp32)
        rs = sb("rs", [P, 1], fp32)
        rq = sb("rq", [P, 1], fp32)
        zb = [sb(f"zb{i}", [P, D], fp32) for i in range(2)]
        lnt = sb("lnt", [P, KD, P], fp32)
        hrow = sb("hrow", [P, D], fp32)

        rec = sb("rec", [P, RECB * BLK * 4], fp32)
        row_id = [sb(f"row_id{j}", [P, SEG], i32) for j in range(BLK // SEG)]
        stage = sb("stage", [P, SLOTS * D], fp32)
        prod = sb("prod", [P, SLOTS * 2 * D], fp16)
        target = sb("target", [P, SLOTS * P], fp16)
        acc = sb("acc", [P, 2, SB, D], fp32)
        xT = [sb(f"xT{i}", [P, KD, P], fp32) for i in range(2)]
        xTh = sb("xTh", [P, 2, KD, SB * P], fp16)
        xTl = sb("xTl", [P, 2, KD, SB * P], fp16)
        h32 = sb("h32", [P, 4, 512], fp32)
        hh = sb("hh", [P, 2, KH, 512], fp16)
        hl = sb("hl", [P, 2, KH, 512], fp16)
        lg = sb("lg", [P, NE], fp32)
        mx = sb("mx", [P, SB, 8], fp32)
        ix = sb("ix", [P, SB, 8], u32)
        ixf = sb("ixf", [P, SB, 2], fp32)
        diff = sb("diff", [P, SB], fp32)
        ex = sb("ex", [P, SB], fp32)
        den = sb("den", [P, SB], fp32)
        tw = sb("tw", [P, SB, 2], fp32)
        iota8 = sb("iota8", [P, SB, NE], fp32)
        eq0 = sb("eq0", [P, SB, NE], fp32)
        eq1 = sb("eq1", [P, SB, NE], fp32)
        wfull = sb("wfull", [P, SB, 32], fp32)
        wT = sb("wT", [P, P], fp32)

        room = prod[:, :].bitcast(fp32)
        dst_i = room[:, 0:CH].bitcast(i32)
        wgt = room[:, CH:2 * CH]
        bucket = room[:, 2 * CH:3 * CH]
        row_in_tile = room[:, 3 * CH:4 * CH]
        src_i = h32[:, :, :].rearrange("p a b -> p (a b)")[:, 0:CH].bitcast(i32)
        zeros_rec = hh[:, :, :, :].rearrange("p a b c -> p (a b c)").bitcast(fp32)[:, 0:928]
        onehot = hl[:, :, :, :].rearrange("p a b c -> p (a b c)").bitcast(bf16)[:, 0:TC * NB].rearrange(
            "p (g c b) -> p g c b", g=NG, c=GC)
        wstage = stage[:, :].rearrange("p (a b) -> p a b", b=KD * HID)
        NWS = wstage.shape[1]

        bank = [ctx.enter_context(nc.psum_tensor(f"bank{i}", [P, 512], fp32)) for i in range(8)]
        psA, psH, psY, psT, psM = bank[0:2], bank[2:4], bank[4:6], bank[6], bank[7]
        ps_count, ps_run = bank[2], bank[0:2]

        s_pad = sem("s_pad")
        s_edges = sem("s_edges")
        s_small = sem("s_small")
        s_b2z = sem("s_b2z")
        s_const = sem("s_const")
        s_constv = sem("s_constv")
        s_wload = [sem(f"s_wload{i}") for i in range(NWS)]
        s_whi = sem("s_whi")
        s_wlo = sem("s_wlo")
        s_wtmp = sem("s_wtmp")
        s_bias = sem("s_bias")
        s_prep = sem("s_prep")
        s_oh = sem("s_oh")
        s_ohused = sem("s_ohused")
        s_counted = sem("s_counted")
        s_tables = sem("s_tables")
        s_run = sem("s_run")
        s_ranks = sem("s_ranks")
        s_read = sem("s_read")
        s_pos = sem("s_pos")
        s_row = sem("s_row")
        s_rec = sem("s_rec")
        s_scat = [sem(f"s_scat{g}") for g in range(NG)]
        s_clear = sem("s_clear")
        s_zt = sem("s_zt")
        s_xload = sem("s_xload")
        s_ln = sem("s_ln")
        s_own = sem("s_own")
        s_lntr = sem("s_lntr")
        s_lnt = sem("s_lnt")
        s_hmm = sem("s_hmm")
        s_hrow = sem("s_hrow")
        s_hst = sem("s_hst")
        s_gate = sem("s_gate")

        s_recl = sem("s_recl")
        s_ids = sem("s_ids")
        s_gat = [sem(f"s_gat{k}") for k in range(SLOTS)]
        s_gath = sem("s_gath")
        s_phi = sem("s_phi")
        s_plo = sem("s_plo")
        s_summed = sem("s_summed")
        s_agg = sem("s_agg")
        s_xl = [sem("s_xl0"), sem("s_xl1")]
        s_x1 = sem("s_x1")
        s_z = sem("s_z")
        s_own3 = sem("s_own3")
        s_tr = sem("s_tr")
        s_xTh = sem("s_xTh")
        s_xTl = sem("s_xTl")
        s_lgm = sem("s_lgm")
        s_lgc = sem("s_lgc")
        s_top = sem("s_top")
        s_diff = sem("s_diff")
        s_exp = sem("s_exp")
        s_fin = sem("s_fin")
        s_wf = sem("s_wf")
        s_wtr = sem("s_wtr")
        s_wT = sem("s_wT")
        s_w1 = sem("s_w1")
        s_hh = sem("s_hh")
        s_hl = sem("s_hl")
        s_y = sem("s_y")
        s_yadd = sem("s_yadd")
        s_ost = sem("s_ost")

        def reached(eng, s, value, gate=True):
            if isinstance(value, int):
                if value > 0:
                    eng.wait_ge(s, value)
                return
            eng.wait_ge(s, value)
            if gate:
                eng.sem_inc(s_gate, 1)

        clear_v = edge_list.rearrange("(p a) c -> p (a c)", p=P)
        NCLR = clear_v.shape[1] // zeros_rec.shape[1]
        assert NCLR * zeros_rec.shape[1] == clear_v.shape[1]

        NSMALL = 4 * KD + NHC + SB + 2
        OWN = 11
        OWN3 = 2 * OWN + 2

        block = ctx.enter_context(nc.Block())

        @block.sync
        def _(sp):
            sp.wait_ge(s_pad, 3)
            for t, a in ((src_i, src), (dst_i, dst), (wgt, edge_weight)):
                sp.dma_start(t[:, 0:COLS], a[0:COLS * P].rearrange("(p c) -> p c", p=P)).then_inc(s_edges, 16)
                sp.dma_start(t[0:LEFT, COLS:COLS + 1],
                             a[COLS * P:E].rearrange("(p c) -> p c", c=1)).then_inc(s_edges, 16)
            sp.wait_ge(s_b2z, 1)
            for k in range(KD):
                sp.dma_start(gam[:, k:k + 1], gamma[k * P:(k + 1) * P].rearrange("(p c) -> p c", c=1)).then_inc(s_small, 16)
                sp.dma_start(bet[:, k:k + 1], beta[k * P:(k + 1) * P].rearrange("(p c) -> p c", c=1)).then_inc(s_small, 16)
                sp.dma_start(wr_t[:, k, :], Wr[k * P:(k + 1) * P, :]).then_inc(s_small, 16)
                sp.dma_start(w_t[:, k, :], gnn_W[k * P:(k + 1) * P, :]).then_inc(s_small, 16)
            for e in range(NE):
                for m in range(KH):
                    sp.dma_start(b1_t[:, e * KH + m:e * KH + m + 1],
                                 b1[e, m * P:(m + 1) * P].rearrange("(p c) -> p c", c=1)).then_inc(s_small, 16)
            for q in range(SB):
                sp.dma_start(b2_t[32 * q:32 * q + NE, q, :], b2[:, :]).then_inc(s_small, 16)
            sp.dma_start(br_t[:, :], br.rearrange("(a n) -> a n", a=1)).then_inc(s_small, 16)
            sp.dma_start(bias_f[:, :], gnn_bias.rearrange("(a n) -> a n", a=1)).then_inc(s_small, 16)
            for n in range(2 * NE):
                e, second = n // 2, n % 2
                if n >= NWS:
                    sp.wait_ge(s_wlo, n - NWS + 1)
                w = (W2[e].rearrange("(k p) n -> p k n", p=P) if second
                     else W1[e].rearrange("(k p) n -> p k n", p=P))
                dst_w = wstage[:, n % NWS, :].rearrange("p (k n) -> p k n", k=KH if second else KD)
                sp.dma_start(dst_w, w).then_inc(s_wload[n % NWS], 16)
            sp.wait_ge(s_zt, 1)
            for i in range(NCLR):
                w_ = zeros_rec.shape[1]
                sp.dma_start(clear_v[:, i * w_:(i + 1) * w_], zeros_rec[:, :]).then_inc(s_clear, 16)

            sp.dma_start(xt[0][PAD:P, :], x[0:P - PAD, :]).then_inc(s_xload, 16)
            reached(sp, s_ln, 1)
            sp.dma_start(xt[0][:, :], x[P - PAD:2 * P - PAD, :]).then_inc(s_xload, 16)
            reached(sp, s_hrow, 1)
            sp.dma_start(h_table[0:P - PAD, :], hrow[PAD:P, :]).then_inc(s_hst, 16)
            with sp.Fori(2, NT) as b:
                reached(sp, s_ln, b)
                sp.dma_start(xt[0][:, :], x[ds(b * P - PAD, P), :]).then_inc(s_xload, 16)
                reached(sp, s_hrow, b)
                sp.dma_start(h_table[ds((b - 1) * P - PAD, P), :], hrow[:, :]).then_inc(s_hst, 16)
            reached(sp, s_hrow, NT)
            sp.dma_start(h_table[(NT - 1) * P - PAD:N, :], hrow[:, :]).then_inc(s_hst, 16)

            sp.wait_ge(s_tables, 1)
            blocks = sp.value_load(blocks_n[0:1, 0:1], min_val=3, max_val=-(-MAXCH // BLK))
            for g in range(NG):
                sp.wait_ge(s_scat[g], 16 * GC * TURNS)
            list_v = edge_list.rearrange("(b p r) c -> b p (r c)", p=P, r=BLK)

            def load_block(b):
                sp.dma_start(rec[:, ds((b % RECB) * BLK * 4, BLK * 4)],
                             list_v[ds(b, 1), :, :].rearrange("b p n -> p (b n)")).then_inc(s_recl, 16)

            def relay(b):
                reached(sp, s_plo, (b - 1) * BLK)
                load_block(b + 1)
                for k in range(SLOTS):
                    reached(sp, s_gat[k], 16 * (b + 1), gate=False)
                    sp.sem_inc(s_gath, 1)
                reached(sp, s_recl, 16 * (b + 2))

            load_block(0)
            sp.wait_ge(s_recl, 16)
            relay(0)
            relay(1)
            with sp.Fori(2, blocks) as b:
                relay(b)

        @block.gpsimd
        def _(pool):
            nc.gpsimd.memset(ident[:, :], 0.0).then_inc(s_const, 1)
            nc.gpsimd.memset(before_b[:, :], 1.0).then_inc(s_const, 1)
            nc.gpsimd.iota(iota_i[:, :], pattern=[[1, P]], base=0, channel_multiplier=0).then_inc(s_const, 1)
            pool.wait_ge(s_const, 3)
            nc.gpsimd.affine_select(out=ident[:, :], in_=ident[:, :], compare_op=ALU.not_equal, fill=1.0,
                                    base=0, pattern=[[-1, P]], channel_multiplier=1).then_inc(s_const, 1)
            nc.gpsimd.affine_select(out=before_b[:, :], in_=before_b[:, :], compare_op=ALU.is_gt, fill=0.0,
                                    base=0, pattern=[[1, P]], channel_multiplier=-1).then_inc(s_const, 1)
            for n in range(2 * NE):
                e, second = n // 2, n % 2
                hi = (w2h if second else w1h)[:, e, :, :].rearrange("p k n -> p (k n)")
                lo = (w2l if second else w1l)[:, e, :, :].rearrange("p k n -> p (k n)")
                slot = wstage[:, n % NWS, :]
                pool.wait_ge(s_whi, n + 1)
                nc.gpsimd.tensor_scalar(slot, slot, WSCALE, None, ALU.mult).then_inc(s_wtmp, 1)
                pool.wait_ge(s_wtmp, n + 1)
                nc.gpsimd.tensor_tensor(lo, slot, hi, ALU.subtract).then_inc(s_wlo, 1)

            pool.wait_ge(s_clear, 16 * NCLR)

            def scatter(i):
                for g in range(NG):
                    reached(pool, s_row, (i * NG + g) + 1)
                    reached(pool, s_rec, (i * NG + g) + 1)
                    for c in range(GC):
                        pool.indirect_dma_start(
                            out=edge_list[:, :], out_offset=bass.IndirectOffsetOnAxis(ap=list_row[g][:, c:c + 1], axis=0),
                            in_=record[g][:, c, :], in_offset=None).then_inc(s_scat[g], 16)

            scatter(0)
            with pool.Fori(1, TURNS) as i:
                scatter(i)

            blocks = pool.value_load(blocks_n[0:1, 0:1], min_val=3, max_val=-(-MAXCH // BLK))
            pool.wait_ge(s_hst, 16 * NT)

            def ids(b, j):
                reached(pool, s_gath, (b - 1) * BLK + (j + 1) * SEG)
                first = ((b % RECB) * BLK + j * SEG) * 4
                nc.gpsimd.tensor_copy(row_id[j][:, :], rec[:, ds(first, SEG * 4)].rearrange(
                    "p (r c) -> p r c", c=4)[:, :, 0]).then_inc(s_ids, 1)

            def gather(b):
                reached(pool, s_recl, 16 * (b + 1))
                ids(b, 0)
                for j in range(BLK // SEG):
                    if j + 1 < BLK // SEG:
                        ids(b, j + 1)
                    reached(pool, s_ids, b * (BLK // SEG) + j + 1)
                    for k in range(j * SEG, (j + 1) * SEG):
                        reached(pool, s_plo, (b - 1) * BLK + k + 1)
                        pool.indirect_dma_start(
                            out=stage[:, k * D:(k + 1) * D], out_offset=None, in_=h_table[:, :],
                            in_offset=bass.IndirectOffsetOnAxis(ap=row_id[j][:, k % SEG:k % SEG + 1], axis=0),
                        ).then_inc(s_gat[k], 16)

            gather(0)
            with pool.Fori(1, blocks) as b:
                gather(b)

        @block.scalar
        def _(act):
            for n in range(2 * NE):
                e, second = n // 2, n % 2
                hi = (w2h if second else w1h)[:, e, :, :].rearrange("p k n -> p (k n)")
                act.wait_ge(s_wload[n % NWS], 16 * (n // NWS + 1))
                nc.scalar.activation(hi, wstage[:, n % NWS, :], ACT.Copy, scale=WSCALE).then_inc(s_whi, 1)
            act.wait_ge(s_small, 16 * NSMALL)
            nc.scalar.activation(bias_hl[0:1, 0:D], bias_f[:, :], ACT.Copy).then_inc(s_bias, 1)

            act.wait_ge(s_tables, 1)

            def turn(i, tile):
                for g in range(NG):
                    reached(act, s_scat[g], 16 * GC * i)
                    col = ds(i * TC + g * GC, GC)
                    nc.scalar.activation(record[g][:, :, 0], dst_i[:, col], ACT.Copy)
                    nc.scalar.activation(record[g][:, :, 1], row_in_tile[:, col], ACT.Copy)
                    nc.scalar.activation(record[g][:, :, 2], wgt[:, col], ACT.Copy).then_inc(s_rec, 1)
                    if tile and g == 1:
                        reached(act, s_lntr, i + 1)
                        reached(act, s_hmm, i)
                        nc.scalar.activation(lnt[:, :, :].rearrange("p k n -> p (k n)"), psT[:, 0:KD * P],
                                             ACT.Copy).then_inc(s_lnt, 1)
                    if tile and g == 3:
                        reached(act, s_hmm, i + 1)
                        reached(act, s_hst, 16 * i)
                        nc.scalar.activation(hrow[:, :], psM[:, 0:D], ACT.Copy).then_inc(s_hrow, 1)

            turn(0, True)
            with act.Fori(1, NT) as i:
                turn(i, True)
            with act.Fori(NT, TURNS) as i:
                turn(i, False)

            act.wait_ge(s_tables, 1)

            def load_x(b, par):
                reached(act, s_x1, b - 1)
                act.dma_start(xt[par][:, :], x[ds(b * P - PAD, P), :]).then_inc(s_xl[par], 16)

            def chunks(b):
                lo_t = act.value_load(start_i[0:1, ds(b, 1)], min_val=0, max_val=MAXCH)
                hi_t = act.value_load(start_i[0:1, ds(b + 1, 1)], min_val=1, max_val=MAXCH)
                with act.Fori(lo_t, hi_t) as t:
                    reached(act, s_gath, t + 1)
                    reached(act, s_summed, t + 1)
                    nc.scalar.activation(prod[:, ds((t % SLOTS) * 2 * D, D)], stage[:, ds((t % SLOTS) * D, D)], ACT.Copy,
                                         scale=rec[:, ds((t % (RECB * BLK)) * 4 + 2, 1)]).then_inc(s_phi, 1)

            def transposed(b, par, spar, q):
                reached(act, s_tr, b + 1)
                reached(act, s_lgm, b - 1)
                reached(act, s_xTl, b - 1)
                for k in range(KD):
                    nc.scalar.activation(xT[par][:, k, :], psT[:, k * P:(k + 1) * P], ACT.Identity,
                                         scale=gam[:, k:k + 1], bias=bet[:, k:k + 1])
                for k in range(KD):
                    last = nc.scalar.activation(xTh[:, spar, k, q * P:(q + 1) * P], psT[:, k * P:(k + 1) * P],
                                                ACT.Identity, scale=gam[:, k:k + 1], bias=bet[:, k:k + 1])
                last.then_inc(s_xTh, 1)

            def gelus(f, e):
                n0 = f * NHC + e * KH
                reached(act, s_y, f * YPS + SB + (e - 2) * SB + SB if e >= 2 else
                        (f - 1) * YPS + SB + (NE - 2 + e) * SB + SB)
                for m in range(KH):
                    reached(act, s_w1, n0 + m + 1)
                    reached(act, s_hl, n0 + m - 3)
                    nc.scalar.activation(h32[:, m, :], psH[m % 2][:, :], ACT.Gelu,
                                         scale=1.0 / WSCALE, bias=b1_t[:, e * KH + m:e * KH + m + 1])
                    nc.scalar.activation(hh[:, e % 2, m, :], psH[m % 2][:, :], ACT.Gelu,
                                         scale=1.0 / WSCALE,
                                         bias=b1_t[:, e * KH + m:e * KH + m + 1]).then_inc(s_hh, 1)

            def exps(s):
                reached(act, s_diff, s + 1)
                nc.scalar.activation(ex[:, :], diff[:, :], ACT.Exp).then_inc(s_exp, 1)

            def weights_T(f):
                reached(act, s_wtr, f + 1)
                nc.scalar.activation(wT[:, :], psM[:, P:2 * P], ACT.Copy).then_inc(s_wT, 1)

            def step(s, q, f, spar, b, more):
                if b is not None:
                    if more:
                        load_x(b + 1, (q + 1) % 2)
                    chunks(b)
                if f is not None:
                    gelus(f, 2 * q)
                    if q == 0:
                        weights_T(f)
                if b is not None:
                    transposed(b, q % 2, spar, q)
                if f is not None:
                    gelus(f, 2 * q + 1)
                if b is not None and q == (SB - 1):
                    exps(s)

            def store(f, fpar):
                reached(act, s_yadd, (f + 1) * YPS)
                if isinstance(f, int) and f == 0:
                    act.dma_start(out[0:P - PAD, :], acc[PAD:P, 0, 0, :]).then_inc(s_ost, 16)
                    act.dma_start(out[P - PAD:2 * P - PAD, :], acc[:, 0, 1, :]).then_inc(s_ost, 16)
                else:
                    r = (2 + (f - 1) * SB) * P - PAD
                    act.dma_start(out[ds(r, SB * P), :].rearrange("(q p) d -> p q d", p=P),
                                  acc[:, fpar, :, :]).then_inc(s_ost, 16)

            act.wait_ge(s_hrow, NT)
            act.dma_start(xt[0][PAD:P, :], x[0:P - PAD, :]).then_inc(s_xl[0], 16)
            act.dma_start(xt[1][:, :], x[P - PAD:2 * P - PAD, :]).then_inc(s_xl[1], 16)
            chunks(0)
            transposed(0, 0, 0, 0)
            load_x(2, 0)
            chunks(1)
            transposed(1, 1, 0, 1)
            exps(0)

            def pair(j, last):
                for h in range(2):
                    s, f = 2 * j + 1 + h, 2 * j + h
                    for q in range(SB):
                        b = 2 + (2 * j + h) * SB + q
                        more = not (last and h == 1 and q == SB - 1)
                        step(s, q, f, 1 - h, b, more)
                    store(f, h)

            pair(0, False)
            with act.Fori(1, NSB // 2 - 1) as j:
                pair(j, False)
            pair(NSB // 2 - 1, True)
            for q in range(SB):
                step(None, q, NSB, None, None, False)
            store(NSB, 0)
            act.wait_ge(s_ost, 16 * (NSB + 2))

        @block.vector
        def _(dve):
            nc.vector.memset(src_i[:, COLS:CH], N).then_inc(s_pad, 1)
            nc.vector.memset(dst_i[:, COLS:CH], 0).then_inc(s_pad, 1)
            nc.vector.memset(wgt[:, COLS:CH], 0.0).then_inc(s_pad, 1)
            nc.vector.memset(b2_t[:, :, :].rearrange("p q d -> p (q d)"), 0.0).then_inc(s_b2z, 1)
            nc.vector.memset(zeros_rec[:, :], 0.0)
            nc.vector.memset(xt[0][:, :], 0.0)
            for g in range(NG):
                last = nc.vector.memset(record[g][:, :, :].rearrange("p c r -> p (c r)"), 0.0)
            last.then_inc(s_zt, 1)
            nc.vector.memset(ones_b[:, :], 1.0)
            nc.vector.memset(ones_f[:, :], 1.0)
            nc.vector.memset(zero_h[:, :], 0.0)
            nc.vector.memset(one_h[:, :], 1.0)
            nc.vector.memset(start_f[:, 0:1], 0.0)
            nc.vector.memset(acc[:, 0, :, :].rearrange("p q d -> p (q d)"), 0.0)
            nc.vector.memset(xTh[:, 0, :, :].rearrange("p k n -> p (k n)"), 0.0)
            nc.vector.memset(xTl[:, 0, :, :].rearrange("p k n -> p (k n)"), 0.0)
            nc.vector.memset(mx[:, :, :].rearrange("p q n -> p (q n)"), 0.0)
            nc.vector.memset(ix[:, :, :].rearrange("p q n -> p (q n)"), 0)
            nc.vector.memset(wfull[:, :, :].rearrange("p q n -> p (q n)"), 0.0)
            dve.wait_ge(s_const, 3)
            nc.vector.tensor_copy(iota_h[:, :], iota_i[:, :])
            for q in range(SB):
                nc.vector.tensor_copy(iota8[:, q, :], iota_i[:, 0:NE])
            nc.vector.tensor_copy(iota_b[:, :], iota_i[:, 0:NB]).then_inc(s_constv, 1)
            dve.wait_ge(s_constv, 1)

            own = [0]

            def then(ins):
                own[0] += 1
                ins.then_inc(s_prep, 1)
                dve.wait_ge(s_prep, own[0])

            dve.wait_ge(s_edges, 16 * 6)
            then(nc.vector.tensor_scalar(src_i[:, :], src_i[:, :], PAD, None, ALU.add))
            row_bits, bucket_bits = row_in_tile[:, :].bitcast(i32), bucket[:, :].bitcast(i32)
            then(nc.vector.tensor_scalar(row_bits, src_i[:, :], P - 1, None, ALU.bitwise_and))
            then(nc.vector.tensor_copy(row_in_tile[:, :], row_bits))
            then(nc.vector.tensor_scalar(bucket_bits, src_i[:, :], 7, None, ALU.logical_shift_right))
            then(nc.vector.tensor_copy(bucket[:, :], bucket_bits))
            dve.wait_ge(s_bias, 1)
            nc.vector.tensor_tensor(bias_hl[0:1, D:2 * D], bias_f[:, :], bias_hl[0:1, 0:D],
                                    ALU.subtract).then_inc(s_bias, 1)
            b2_all = b2_t[:, :, :].rearrange("p q d -> p (q d)")
            nc.vector.tensor_scalar(b2_all, b2_all, WSCALE, None, ALU.mult).then_inc(s_bias, 1)

            def build(i, g, used):
                reached(dve, used, (i - 1) * NG + g + 1, gate=False)
                for c in range(GC):
                    last = nc.vector.tensor_scalar(onehot[:, g, c, :], iota_b[:, :],
                                                   bucket[:, ds(i * TC + g * GC + c, 1)], None, ALU.is_equal)
                last.then_inc(s_oh, 1)

            for g in range(NG):
                build(0, g, s_ohused)
            with dve.Fori(1, TURNS) as i:
                for g in range(NG):
                    build(i, g, s_ohused)

            dve.wait_ge(s_counted, 1)
            then(nc.vector.tensor_reduce(cnt_f[:, :], ps_count[:, 0:GC * NB].rearrange("p (c b) -> p b c", c=GC),
                                         AX.X, ALU.add))
            then(nc.vector.tensor_scalar(cnt_i[:, :], cnt_f[:, :], float(P - 1), None, ALU.add))
            then(nc.vector.tensor_scalar(nch_i[:, :], cnt_i[:, :], 7, None, ALU.logical_shift_right))
            then(nc.vector.tensor_scalar(nch_f[:, :], nch_i[:, :], 1.0, None, ALU.max))
            then(nc.vector.tensor_tensor_scan(start_f[:, 1:NB + 1], ones_f[:, 0:NB], nch_f[:, :], 0.0,
                                              ALU.mult, ALU.add))
            then(nc.vector.tensor_copy(start_i[:, :], start_f[:, :]))
            then(nc.vector.tensor_scalar(run_row[0:1, 0, :], start_f[0:1, 0:NB], float(P), None, ALU.mult))
            then(nc.vector.tensor_scalar(blocks_i[:, :], start_f[:, NT:NT + 1], float(BLK - 1), None, ALU.add))
            then(nc.vector.tensor_scalar(blocks_n[:, :], blocks_i[:, :], 5, None, ALU.logical_shift_right))
            dve.sem_inc(s_tables, 1)

            def normalise(out_ap, in_ap, s, base):
                nc.vector.bn_stats(stats[:, :], in_ap).then_inc(s, 1)
                reached(dve, s, base + 1)
                nc.vector.bn_aggr(mv[:, :], stats[:, :]).then_inc(s, 1)
                reached(dve, s, base + 2, gate=False)
                nc.vector.tensor_scalar(ve[:, :], mv[:, 1:2], EPS, None, ALU.add).then_inc(s, 1)
                reached(dve, s, base + 3, gate=False)
                nc.vector.tensor_scalar(rs[:, :].bitcast(i32), ve[:, :].bitcast(i32), -0.5, float(0x5F3759DF),
                                        ALU.mult, ALU.add).then_inc(s, 1)
                nc.vector.tensor_scalar(vh[:, :], ve[:, :], -0.5, None, ALU.mult).then_inc(s, 1)
                for k in range(3):
                    reached(dve, s, base + 5 + 2 * k, gate=False)
                    nc.vector.scalar_tensor_tensor(rq[:, :], rs[:, :], rs[:, 0:1], vh[:, :], ALU.mult,
                                                   ALU.mult).then_inc(s, 1)
                    reached(dve, s, base + 6 + 2 * k, gate=False)
                    nc.vector.scalar_tensor_tensor(rs[:, :], rq[:, :], 1.5, rs[:, :], ALU.add,
                                                   ALU.mult).then_inc(s, 1)
                reached(dve, s, base + OWN, gate=False)
                return nc.vector.tensor_scalar(out_ap, in_ap, mv[:, 0:1], rs[:, 0:1], ALU.subtract, ALU.mult)

            def select(i, g):
                reached(dve, s_read, i * NG + g, gate=False)
                reached(dve, s_ranks, i * NG + g + 1, gate=False)
                nc.vector.tensor_copy(run_row[0:1, 0, :],
                                      ps_run[g % 2][0:1, GC * NB:(GC + 1) * NB]).then_inc(s_run, 1)
                for c in range(GC):
                    last = nc.vector.scalar_tensor_tensor(
                        chosen[:, c, :], ps_run[g % 2][:, c * NB:(c + 1) * NB], 1.0, onehot[:, g, c, :], ALU.mult, ALU.mult,
                        accum_out=pos_f[:, g * GC + c:g * GC + c + 1])
                last.then_inc(s_read, 1)

            def turn(i, tile):
                build(i, 0, s_ranks)
                for g in range(NG):
                    if g + 1 < NG:
                        build(i, g + 1, s_ranks)
                    select(i, g)
                    if tile and g == 0:
                        reached(dve, s_xload, 16 * (i + 1))
                        reached(dve, s_lntr, i)
                        normalise(zb[0][:, :], xt[0][:, :], s_own, OWN * i).then_inc(s_ln, 1)
                reached(dve, s_read, (i + 1) * NG, gate=False)
                nc.vector.tensor_copy(pos_i[:, :], pos_f[:, :]).then_inc(s_pos, 1)
                reached(dve, s_pos, 5 * i + 1, gate=False)
                nc.vector.tensor_scalar(pos_a[:, :], pos_i[:, :], -BLK * P, None, ALU.bitwise_and).then_inc(s_pos, 1)
                nc.vector.tensor_scalar(pos_b[:, :], pos_i[:, :], P - 1, 5, ALU.bitwise_and,
                                        ALU.logical_shift_left).then_inc(s_pos, 1)
                nc.vector.tensor_scalar(pos_c[:, :], pos_i[:, :], 7, BLK - 1, ALU.logical_shift_right,
                                        ALU.bitwise_and).then_inc(s_pos, 1)
                reached(dve, s_pos, 5 * i + 4, gate=False)
                nc.vector.tensor_tensor(pos_b[:, :], pos_b[:, :], pos_c[:, :], ALU.bitwise_or).then_inc(s_pos, 1)
                reached(dve, s_pos, 5 * i + 5, gate=False)
                for g in range(NG):
                    reached(dve, s_scat[g], 16 * GC * i, gate=False)
                    nc.vector.tensor_tensor(list_row[g][:, :], pos_a[:, g * GC:(g + 1) * GC],
                                            pos_b[:, g * GC:(g + 1) * GC], ALU.bitwise_or).then_inc(s_row, 1)

            turn(0, True)
            with dve.Fori(1, NT) as i:
                turn(i, True)
            with dve.Fori(NT, TURNS) as i:
                turn(i, False)

            def chunks(b):
                lo_t = dve.value_load(start_i[0:1, ds(b, 1)], min_val=0, max_val=MAXCH)
                hi_t = dve.value_load(start_i[0:1, ds(b + 1, 1)], min_val=1, max_val=MAXCH)
                with dve.Fori(lo_t, hi_t) as t:
                    reached(dve, s_phi, t + 1, gate=False)
                    nc.vector.tensor_scalar(target[:, ds((t % SLOTS) * P, P)], iota_h[:, :],
                                            rec[:, ds((t % (RECB * BLK)) * 4 + 1, 1)], None, ALU.is_equal)
                    nc.vector.scalar_tensor_tensor(
                        prod[:, ds((t % SLOTS) * 2 * D + D, D)], stage[:, ds((t % SLOTS) * D, D)],
                        rec[:, ds((t % (RECB * BLK)) * 4 + 2, 1)], prod[:, ds((t % SLOTS) * 2 * D, D)],
                        ALU.mult, ALU.subtract).then_inc(s_plo, 1)

            def epilogue(b, par, spar, q, loads, s):
                rows = acc[:, spar, q, :]
                reached(dve, s_agg, b + 1, gate=False)
                reached(dve, s_xl[par], 16 * loads, gate=False)
                if not isinstance(s, int) or s > 1:
                    reached(dve, s_ost, 16 * s, gate=False)
                nc.vector.tensor_tensor(rows, xt[par][:, :], psA[par][:, 0:D], ALU.add).then_inc(s_own3, 1)
                reached(dve, s_own3, OWN3 * b + 1, gate=False)
                nc.vector.tensor_tensor(rows, rows, psA[par][:, D:2 * D], ALU.add).then_inc(s_x1, 1)
                reached(dve, s_x1, b + 1, gate=False)
                normalise(z1[:, :], rows, s_own3, OWN3 * b + 1).then_inc(s_own3, 1)
                reached(dve, s_own3, OWN3 * b + 2 + OWN, gate=False)
                reached(dve, s_tr, b - 1, gate=False)
                normalise(zb[par][:, :], z1[:, :], s_own3, OWN3 * b + 2 + OWN).then_inc(s_z, 1)

            def x_low(b, par, spar, q):
                reached(dve, s_xTh, b + 1, gate=False)
                nc.vector.tensor_tensor(xTl[:, spar, :, q * P:(q + 1) * P], xT[par][:, :, :],
                                        xTh[:, spar, :, q * P:(q + 1) * P], ALU.subtract).then_inc(s_xTl, 1)

            def top2(b, q):
                reached(dve, s_lgm, b + 1, gate=False)
                nc.vector.tensor_copy(lg[:, :], psM[:, 0:NE]).then_inc(s_lgc, 1)
                reached(dve, s_lgc, b + 1)
                nc.vector.max(mx[:, q, :], lg[:, :]).then_inc(s_top, 1)
                reached(dve, s_top, 2 * b + 1)
                nc.vector.max_index(ix[:, q, :], mx[:, q, :], lg[:, :]).then_inc(s_top, 1)

            def finalise(s):
                base = 8 * s
                reached(dve, s_top, 2 * (SB * s + 2), gate=False)
                nc.vector.tensor_tensor(diff[:, :], mx[:, :, 1], mx[:, :, 0], ALU.subtract).then_inc(s_diff, 1)
                nc.vector.tensor_copy(ixf[:, :, :], ix[:, :, 0:2]).then_inc(s_fin, 1)
                reached(dve, s_exp, s + 1, gate=False)
                nc.vector.tensor_scalar(den[:, :], ex[:, :], 1.0, WSCALE, ALU.add, ALU.mult).then_inc(s_fin, 1)
                reached(dve, s_fin, base + 2, gate=False)
                nc.vector.reciprocal(tw[:, :, 0], den[:, :]).then_inc(s_fin, 1)
                reached(dve, s_fin, base + 3, gate=False)
                nc.vector.tensor_tensor(tw[:, :, 1], ex[:, :], tw[:, :, 0], ALU.mult).then_inc(s_fin, 1)
                for k, eq in enumerate((eq0, eq1)):
                    nc.vector.tensor_tensor(eq[:, :, :], iota8[:, :, :], ixf[:, :, k:k + 1].to_broadcast([P, SB, NE]),
                                            ALU.is_equal).then_inc(s_fin, 1)
                reached(dve, s_fin, base + 6, gate=False)
                for k, eq in enumerate((eq0, eq1)):
                    nc.vector.tensor_tensor(eq[:, :, :], eq[:, :, :], tw[:, :, k:k + 1].to_broadcast([P, SB, NE]),
                                            ALU.mult).then_inc(s_fin, 1)
                reached(dve, s_fin, base + 8, gate=False)
                reached(dve, s_wtr, s, gate=False)
                nc.vector.tensor_tensor(wfull[:, :, 0:NE], eq0[:, :, :], eq1[:, :, :], ALU.add).then_inc(s_wf, 1)

            def h_low(f, e):
                for m in range(KH):
                    reached(dve, s_hh, f * NHC + e * KH + m + 1, gate=False)
                    nc.vector.tensor_tensor(hl[:, e % 2, m, :], h32[:, m, :], hh[:, e % 2, m, :],
                                            ALU.subtract).then_inc(s_hl, 1)

            def add_b2(f, fpar):
                reached(dve, s_wf, f + 1, gate=False)
                for q in range(SB):
                    reached(dve, s_y, f * YPS + q + 1, gate=False)
                    nc.vector.tensor_tensor(acc[:, fpar, q, :], acc[:, fpar, q, :], psY[q % 2][:, 0:D],
                                            ALU.add).then_inc(s_yadd, 1)

            def add_expert(f, fpar, e):
                for q in range(SB):
                    y = f * YPS + SB + e * SB + q
                    reached(dve, s_y, y + 1, gate=False)
                    reached(dve, s_yadd, y - SB + 1, gate=False)
                    nc.vector.scalar_tensor_tensor(acc[:, fpar, q, :], psY[q % 2][:, 0:D], wfull[:, q, e:e + 1],
                                                   acc[:, fpar, q, :], ALU.mult, ALU.add).then_inc(s_yadd, 1)

            def step(s, q, f, spar, b, loads):
                if b is not None:
                    chunks(b)
                    epilogue(b, q % 2, spar, q, loads, s)
                if f is not None:
                    h_low(f, 2 * q)
                    if q == 0:
                        add_b2(f, 1 - spar)
                    else:
                        add_expert(f, 1 - spar, 2 * q - 1)
                if b is not None:
                    x_low(b, q % 2, spar, q)
                if f is not None:
                    h_low(f, 2 * q + 1)
                    add_expert(f, 1 - spar, 2 * q)
                if b is not None:
                    top2(b, q)
                if f is not None and q == SB - 1:
                    add_expert(f, 1 - spar, 2 * q + 1)
                if b is not None and q == (1 if f is None else SB - 1):
                    finalise(s)

            for q in range(2):
                step(0, q, None, 0, q, 1)

            def pair(j):
                for h in range(2):
                    for q in range(SB):
                        b = 2 + (2 * j + h) * SB + q
                        step(2 * j + 1 + h, q, 2 * j + h, 1 - h, b, 2 + 4 * j + 2 * h + q // 2)

            pair(0)
            with dve.Fori(1, NSB // 2) as j:
                pair(j)
            for q in range(SB):
                step(None, q, NSB, 1, None, None)

        @block.tensor
        def _(pe):
            pe.wait_ge(s_constv, 1)
            flat = [onehot[:, g, :, :].rearrange("p c b -> p (c b)") for g in range(NG)]
            NG_B = GC * NB

            nc.tensor.matmul(ps_count[:, 0:NG_B], zero_h[:, 0:P], zero_h[:, 0:NG_B], start=True, stop=False)

            def count(i):
                for g in range(NG):
                    reached(pe, s_oh, i * NG + g + 1)
                    nc.tensor.matmul(ps_count[:, 0:NG_B], ones_b[:, :], flat[g], start=False,
                                     stop=False).then_inc(s_ohused, 1)

            count(0)
            with pe.Fori(1, TURNS) as i:
                count(i)
            nc.tensor.matmul(ps_count[:, 0:NG_B], zero_h[:, 0:P], zero_h[:, 0:NG_B], start=False,
                             stop=True).then_inc(s_counted, 1)

            GROUPS = TURNS * NG
            pe.wait_ge(s_tables, 1)

            def turn(i, tile):
                for g in range(NG):
                    group = i * NG + g
                    reached(pe, s_oh, GROUPS + group + 1)
                    reached(pe, s_run, group)
                    reached(pe, s_read, group - 1)
                    ps = ps_run[g % 2]
                    copies = ps[:, 0:(GC + 1) * NB].rearrange("p (c b) -> p c b", b=NB)
                    nc.tensor.matmul(copies, ones_f[0:1, 0:P], run_row[0:1, :, :].to_broadcast([1, GC + 1, NB]),
                                     start=True, stop=False)
                    for c in range(GC):
                        n = GC - c
                        nc.tensor.matmul(copies[:, c + 1:, :], ones_b[:, :],
                                         onehot[:, g, c:c + 1, :].to_broadcast([P, n, NB]), start=False, stop=False)
                    nc.tensor.matmul(ps[:, 0:NG_B], before_b[:, :], flat[g], start=False,
                                     stop=True).then_inc(s_ranks, 1)
                    if tile and g == 1:
                        reached(pe, s_ln, i + 1)
                        reached(pe, s_lnt, i)
                        for k in range(KD):
                            last = nc.tensor.transpose(psT[:, k * P:(k + 1) * P], zb[0][:, k * P:(k + 1) * P], ident[:, :])
                        last.then_inc(s_lntr, 1)
                    if tile and g == 2:
                        reached(pe, s_lnt, i + 1)
                        reached(pe, s_hrow, i)
                        for k in range(KD):
                            last = nc.tensor.matmul(psM[:, 0:D], lnt[:, k, :], w_t[:, k, :], start=(k == 0),
                                                    stop=(k == KD - 1))
                        last.then_inc(s_hmm, 1)

            pe.wait_ge(s_small, 16 * NSMALL)
            turn(0, True)
            with pe.Fori(1, NT) as i:
                turn(i, True)
            with pe.Fori(NT, TURNS) as i:
                turn(i, False)

            pe.wait_ge(s_bias, 3)
            pe.wait_ge(s_wlo, 2 * NE)
            pe.wait_ge(s_hrow, NT)
            pe.wait_ge(s_read, TURNS * NG)
            pe.sem_inc(s_summed, SLOTS)

            def chunks(b, par):
                reached(pe, s_x1, b - 1)
                nc.tensor.matmul(psA[par][:, :], one_h[:, :], bias_hl[:, :], start=True, stop=False)
                lo_t = pe.value_load(start_i[0:1, ds(b, 1)], min_val=0, max_val=MAXCH)
                hi_t = pe.value_load(start_i[0:1, ds(b + 1, 1)], min_val=1, max_val=MAXCH)
                with pe.Fori(lo_t, hi_t) as t:
                    reached(pe, s_plo, t + 1)
                    nc.tensor.matmul(psA[par][:, :], target[:, ds((t % SLOTS) * P, P)],
                                     prod[:, ds((t % SLOTS) * 2 * D, 2 * D)], start=False,
                                     stop=False).then_inc(s_summed, 1)
                nc.tensor.matmul(psA[par][:, :], zero_h[:, 0:P], zero_h[:, :], start=False,
                                 stop=True).then_inc(s_agg, 1)

            def transposes(b, par):
                reached(pe, s_z, b + 1)
                reached(pe, s_xTh, b)
                for k in range(KD):
                    last = nc.tensor.transpose(psT[:, k * P:(k + 1) * P], zb[par][:, k * P:(k + 1) * P], ident[:, :])
                last.then_inc(s_tr, 1)

            def logits(b, par):
                reached(pe, s_xTh, b + 1)
                reached(pe, s_lgc, b)
                nc.tensor.matmul(psM[:, 0:NE], ones_f[0:1, 0:P], br_t[:, :], start=True, stop=False)
                for k in range(KD):
                    last = nc.tensor.matmul(psM[:, 0:NE], xT[par][:, k, :], wr_t[:, k, :], start=False,
                                            stop=(k == KD - 1))
                last.then_inc(s_lgm, 1)

            def hidden(f, fpar, e):
                for m in range(KH):
                    reached(pe, s_hh, f * NHC + e * KH + m - 1)
                    col = slice(m * P, (m + 1) * P)
                    for k in range(KD):
                        wh, wl = w1h[:, e, k, col], w1l[:, e, k, col]
                        xh, xl = xTh[:, fpar, k, :], xTl[:, fpar, k, :]
                        for n, (a, c) in enumerate(((wh, xh), (wh, xl), (wl, xh))):
                            last = nc.tensor.matmul(psH[m % 2][:, :], a, c, start=(k == 0 and n == 0),
                                                    stop=(k == KD - 1 and n == 2))
                    last.then_inc(s_w1, 1)

            def expert(f, e):
                reached(pe, s_hl, f * NHC + (e + 1) * KH)
                for q in range(SB):
                    reached(pe, s_yadd, f * YPS + SB + e * SB + q - 1)
                    rows = slice(q * P, (q + 1) * P)
                    for m in range(KH):
                        ah, al = hh[:, e % 2, m, rows], hl[:, e % 2, m, rows]
                        for n, (a, c) in enumerate(((ah, w2h), (ah, w2l), (al, w2h))):
                            last = nc.tensor.matmul(psY[q % 2][:, 0:D], a, c[:, e, m, :], start=(m == 0 and n == 0),
                                                    stop=(m == KH - 1 and n == 2))
                    last.then_inc(s_y, 1)

            def b2_terms(f):
                reached(pe, s_wf, f + 1)
                reached(pe, s_wT, f)
                nc.tensor.transpose(psM[:, P:2 * P], wfull[:, :, :].rearrange("p q e -> p (q e)"),
                                    ident[:, :]).then_inc(s_wtr, 1)
                reached(pe, s_wT, f + 1)
                for q in range(SB):
                    reached(pe, s_yadd, f * YPS + q - 1)
                    nc.tensor.matmul(psY[q % 2][:, 0:D], wT[:, :], b2_t[:, q, :], start=True,
                                     stop=True).then_inc(s_y, 1)

            def step(q, f, spar, b):
                if b is not None:
                    chunks(b, q % 2)
                if f is not None:
                    if q == 0:
                        reached(pe, s_xTl, SB * f + 2)
                    hidden(f, 1 - spar, 2 * q)
                    if q == 0:
                        b2_terms(f)
                    else:
                        expert(f, 2 * q - 1)
                if b is not None:
                    transposes(b, q % 2)
                if f is not None:
                    hidden(f, 1 - spar, 2 * q + 1)
                    expert(f, 2 * q)
                if b is not None:
                    logits(b, q % 2)
                if f is not None and q == SB - 1:
                    expert(f, 2 * q + 1)

            for q in range(2):
                step(q, None, 0, q)

            def pair(j):
                for h in range(2):
                    for q in range(SB):
                        step(q, 2 * j + h, 1 - h, 2 + (2 * j + h) * SB + q)

            pair(0)
            with pe.Fori(1, NSB // 2) as j:
                pair(j)
            for q in range(SB):
                step(q, NSB, 1, None)


_INS = ["x", "src", "dst", "edge_weight", "L0_gnn_W", "L0_gnn_bias", "L0_ffn_gamma", "L0_ffn_beta", "L0_ffn_Wr",
        "L0_ffn_br", "L0_ffn_W1", "L0_ffn_b1", "L0_ffn_W2", "L0_ffn_b2"]


def kernel(**inputs):
    import numpy as _np
    import concourse.bacc as _bacc
    from concourse import mybir as _mybir
    from concourse.bass_utils import run_bass_kernel_spmd as _run

    nc = _bacc.Bacc("TRN2", target_bir_lowering=False, num_devices=1)
    arrays, args = {}, []
    for name in _INS:
        a = _np.ascontiguousarray(inputs[name])
        arrays[f"in_{name}_dram"] = a
        args.append(nc.dram_tensor(f"in_{name}_dram", a.shape, _mybir.dt.from_np(a.dtype), kind="ExternalInput").ap())
    f32 = _mybir.dt.float32
    rows, cols = inputs["x"].shape
    h_table = nc.dram_tensor("h_table", (rows, cols), f32).ap()
    edge_list = nc.dram_tensor("edge_list", (58 * 4096, 4), f32).ap()
    out = nc.dram_tensor("out_0_dram", (rows, cols), f32, kind="ExternalOutput").ap()
    gnn_moe_layer_kernel(nc, *args, h_table, edge_list, out)
    r = _run(nc, [arrays], core_ids=[0])
    return r.results[0]["out_0_dram"]
```

```python
import concourse.bass as bass
from concourse import mybir
from contextlib import ExitStack


def gnn_moe_layer_kernel(
    nc: bass.Bass,
    x: bass.AP,
    src: bass.AP,
    dst: bass.AP,
    edge_weight: bass.AP,
    gnn_W: bass.AP,
    gnn_bias: bass.AP,
    gamma: bass.AP,
    beta: bass.AP,
    Wr: bass.AP,
    br: bass.AP,
    W1: bass.AP,
    b1: bass.AP,
    W2: bass.AP,
    b2: bass.AP,
    h_table: bass.AP,
    edge_list: bass.AP,
    out: bass.AP,
):
    fp32 = mybir.dt.float32
    fp16 = mybir.dt.float16
    bf16 = mybir.dt.bfloat16
    i32 = mybir.dt.int32
    u32 = mybir.dt.uint32
    ALU = mybir.AluOpType
    ACT = mybir.ActivationFunctionType
    AX = mybir.AxisListType
    ds = bass.ds

    P = 128
    N, D = x.shape
    E = src.shape[0]
    NE, _, HID = W1.shape
    KD = D // P
    KH = HID // P
    NT = -(-N // P)
    PAD = NT * P - N
    EPS = 1e-5
    WSCALE = 64.0

    GC = 4
    NG = 4
    TC = GC * NG
    COLS = E // P
    LEFT = E - COLS * P
    TURNS = -(-(COLS + (LEFT > 0)) // TC)
    CH = TURNS * TC
    NB = NT + 2
    assert NB * GC <= 512 and NT < TURNS and PAD > 0

    BLK = 32
    SEG = 8
    RECB = 4
    QC = 4
    QROWS = QC * P
    MAXQ = E // QROWS + 1 + NT
    SLOTS = 32
    RQ = SLOTS // QC
    GQ = 2
    RG = RQ // GQ
    assert BLK == SLOTS and -(-MAXQ // RQ) + 1 <= edge_list.shape[0] // (BLK * P)
    assert QROWS == 512 and RQ == 8 and GQ == 2

    SB = 4
    NSB = (NT - 2) // SB
    assert NT == 2 + SB * NSB and NSB % 2 == 0
    NHC = NE * KH
    YPS = SB * NE + SB
    assert YPS % 3 == 0

    ctx = ExitStack()
    with ctx:
        ctx.enter_context(nc.allow_non_contiguous_dma(reason="small constants, one element per row"))

        def sb(name, shape, dt):
            return ctx.enter_context(nc.sbuf_tensor(name, shape, dt))

        def sem(name):
            return ctx.enter_context(nc.semaphore(name))

        chosen = sb("chosen", [P, GC, NB], fp32)
        w_high = sb("w_high", [P, CH], fp16)
        pos_f = sb("pos_f", [P, TC], fp32)
        pos_i = sb("pos_i", [P, TC], i32)
        pos_a = sb("pos_a", [P, TC], i32)
        pos_b = sb("pos_b", [P, TC], i32)
        pos_c = sb("pos_c", [P, TC], i32)
        list_row = [sb(f"list_row{g}", [P, GC], i32) for g in range(NG)]
        record = [sb(f"record{g}", [P, GC, 4], fp32) for g in range(NG)]

        cnt_f = sb("cnt_f", [P, NB], fp32)
        cnt_i = sb("cnt_i", [P, NB], i32)
        nch_i = sb("nch_i", [P, NB], i32)
        nch_f = sb("nch_f", [P, NB], fp32)
        ones_f = sb("ones_f", [P, P], fp32)
        start_f = sb("start_f", [P, NB + 1], fp32)
        start_i = sb("start_i", [P, NB + 1], i32)
        some_i = sb("some_i", [P, NB + 1], i32)
        gstart_i = sb("gstart_i", [P, NB + 1], i32)
        gahead_i = sb("gahead_i", [P, NB], i32)
        run_row = sb("run_row", [1, 1, NB], fp32)
        blocks_f = sb("blocks_f", [P, 1], fp32)
        blocks_i = sb("blocks_i", [P, 1], i32)
        blocks_n = sb("blocks_n", [P, 1], i32)

        ident = sb("ident", [P, P], fp32)
        iota_i = sb("iota_i", [P, P], i32)
        iota_h = sb("iota_h", [P, P], fp16)
        iota_b = sb("iota_b", [P, NB], bf16)
        ones_b = sb("ones_b", [P, P], bf16)
        before_b = sb("before_b", [P, P], bf16)
        zero_h = sb("zero_h", [1, 512], fp16)
        one_h = sb("one_h", [1, P], fp16)
        bias_f = sb("bias_f", [1, D], fp32)
        bias_hl = sb("bias_hl", [1, 2 * D], fp16)
        gam = sb("gam", [P, KD], fp32)
        bet = sb("bet", [P, KD], fp32)
        b1_t = sb("b1_t", [P, NHC], fp32)
        wr_t = sb("wr_t", [P, KD, NE], fp32)
        br_t = sb("br_t", [1, NE], fp32)
        b2_t = sb("b2_t", [P, SB, D], fp32)
        w_t = sb("w_t", [P, KD, D], fp32)
        w1h = sb("w1h", [P, NE, KD, HID], fp16)
        w1l = sb("w1l", [P, NE, KD, HID], fp16)
        w2h = sb("w2h", [P, NE, KH, D], fp16)
        w2l = sb("w2l", [P, NE, KH, D], fp16)

        xt = [sb(f"xt{i}", [P, D], fp32) for i in range(2)]
        stats = sb("stats", [P, 6], fp32)
        mv = sb("mv", [P, 2], fp32)
        ve = sb("ve", [P, 1], fp32)
        vh = sb("vh", [P, 1], fp32)
        rs = sb("rs", [P, 1], fp32)
        rq = sb("rq", [P, 1], fp32)
        zb = [sb(f"zb{i}", [P, D], fp32) for i in range(2)]
        lnt = sb("lnt", [P, KD, P], fp32)
        hrow = sb("hrow", [P, D], fp32)
        hrow_hl = sb("hrow_hl", [P, 2 * D], fp16)

        rec = sb("rec", [P, RECB * BLK * 4], fp32)
        row_id = [sb(f"row_id{j}", [P, SEG], i32) for j in range(BLK // SEG)]
        stage = sb("stage", [P, SLOTS * 2 * D], fp16)
        room = sb("room", [P, 4 * CH], fp32)
        acc = sb("acc", [P, 2, SB, D], fp32)
        xT = [sb(f"xT{i}", [P, KD, P], fp32) for i in range(2)]
        xTh = sb("xTh", [P, 2, KD, SB * P], fp16)
        xTl = sb("xTl", [P, 2, KD, SB * P], fp16)
        h32 = sb("h32", [P, 4, 512], fp32)
        hh = sb("hh", [P, 2, KH, 512], fp16)
        hl = sb("hl", [P, 2, KH, 512], fp16)
        lg = sb("lg", [P, NE], fp32)
        mx = sb("mx", [P, SB, 8], fp32)
        ix = sb("ix", [P, SB, 8], u32)
        ixf = sb("ixf", [P, SB, 2], fp32)
        diff = sb("diff", [P, SB], fp32)
        ex = sb("ex", [P, SB], fp32)
        den = sb("den", [P, SB], fp32)
        tw = sb("tw", [P, SB, 2], fp32)
        iota8 = sb("iota8", [P, SB, NE], fp32)
        eq0 = sb("eq0", [P, SB, NE], fp32)
        eq1 = sb("eq1", [P, SB, NE], fp32)
        wfull = sb("wfull", [P, SB, 32], fp32)
        wT = sb("wT", [P, P], fp32)

        target = room[:, 0:SLOTS * P].bitcast(fp16)
        dst_i = room[:, 0:CH].bitcast(i32)
        wgt = room[:, CH:2 * CH]
        bucket = room[:, 2 * CH:3 * CH]
        row_in_tile = room[:, 3 * CH:4 * CH]
        src_i = h32[:, :, :].rearrange("p a b -> p (a b)")[:, 0:CH].bitcast(i32)
        zeros_rec = hh[:, :, :, :].rearrange("p a b c -> p (a b c)").bitcast(fp32)[:, 0:1056]
        onehot = hl[:, :, :, :].rearrange("p a b c -> p (a b c)").bitcast(bf16)[:, 0:TC * NB].rearrange(
            "p (g c b) -> p g c b", g=NG, c=GC)
        wstage = stage[:, :].bitcast(fp32).rearrange("p (a b) -> p a b", b=KD * HID)
        NWS = wstage.shape[1]

        bank = [ctx.enter_context(nc.psum_tensor(f"bank{i}", [P, 512], fp32)) for i in range(8)]
        psA, psH, psY, psT, psM = bank[0], bank[2:4], [bank[4], bank[5], bank[1]], bank[6], bank[7]
        ps_count, ps_run = bank[2], bank[0:2]

        s_pad = sem("s_pad")
        s_edges = sem("s_edges")
        s_small = sem("s_small")
        s_b2z = sem("s_b2z")
        s_const = sem("s_const")
        s_constv = sem("s_constv")
        s_wload = [sem(f"s_wload{i}") for i in range(NWS)]
        s_whi = sem("s_whi")
        s_wlo = sem("s_wlo")
        s_wtmp = sem("s_wtmp")
        s_bias = sem("s_bias")
        s_prep = sem("s_prep")
        s_oh = sem("s_oh")
        s_ohused = sem("s_ohused")
        s_counted = sem("s_counted")
        s_tables = sem("s_tables")
        s_run = sem("s_run")
        s_ranks = sem("s_ranks")
        s_read = sem("s_read")
        s_pos = sem("s_pos")
        s_row = sem("s_row")
        s_rec = sem("s_rec")
        s_scat = [sem(f"s_scat{g}") for g in range(NG)]
        s_clear = sem("s_clear")
        s_zt = sem("s_zt")
        s_xload = sem("s_xload")
        s_ln = sem("s_ln")
        s_own = sem("s_own")
        s_lntr = sem("s_lntr")
        s_lnt = sem("s_lnt")
        s_hmm = sem("s_hmm")
        s_hrow = sem("s_hrow")
        s_hhl = sem("s_hhl")
        s_hst = sem("s_hst")
        s_gate = sem("s_gate")

        s_recl = sem("s_recl")
        s_ids = sem("s_ids")
        s_gat = [sem(f"s_gat{k}") for k in range(SLOTS)]
        s_gath = sem("s_gath")
        s_tgt = sem("s_tgt")
        s_summed = sem("s_summed")
        s_agg = sem("s_agg")
        s_xl = [sem("s_xl0"), sem("s_xl1")]
        s_x1 = sem("s_x1")
        s_z = sem("s_z")
        s_own3 = sem("s_own3")
        s_tr = sem("s_tr")
        s_xTh = sem("s_xTh")
        s_xTl = sem("s_xTl")
        s_lgm = sem("s_lgm")
        s_lgc = sem("s_lgc")
        s_top = sem("s_top")
        s_diff = sem("s_diff")
        s_exp = sem("s_exp")
        s_fin = sem("s_fin")
        s_wf = sem("s_wf")
        s_wtr = sem("s_wtr")
        s_wT = sem("s_wT")
        s_w1 = sem("s_w1")
        s_hh = sem("s_hh")
        s_hl = sem("s_hl")
        s_y = sem("s_y")
        s_yadd = sem("s_yadd")
        s_ost = sem("s_ost")

        def reached(eng, s, value, gate=True):
            if isinstance(value, int):
                if value > 0:
                    eng.wait_ge(s, value)
                return
            eng.wait_ge(s, value)
            if gate:
                eng.sem_inc(s_gate, 1)

        clear_v = edge_list.rearrange("(p a) c -> p (a c)", p=P)
        NCLR = clear_v.shape[1] // zeros_rec.shape[1]
        assert NCLR * zeros_rec.shape[1] == clear_v.shape[1]

        NSMALL = 4 * KD + NHC + SB + 2
        OWN = 11
        OWN3 = OWN + 1

        block = ctx.enter_context(nc.Block())

        @block.sync
        def _(sp):
            sp.wait_ge(s_pad, 3)
            for t, a in ((src_i, src), (dst_i, dst), (wgt, edge_weight)):
                sp.dma_start(t[:, 0:COLS], a[0:COLS * P].rearrange("(p c) -> p c", p=P)).then_inc(s_edges, 16)
                sp.dma_start(t[0:LEFT, COLS:COLS + 1],
                             a[COLS * P:E].rearrange("(p c) -> p c", c=1)).then_inc(s_edges, 16)
            sp.wait_ge(s_b2z, 1)
            for k in range(KD):
                sp.dma_start(gam[:, k:k + 1], gamma[k * P:(k + 1) * P].rearrange("(p c) -> p c", c=1)).then_inc(s_small, 16)
                sp.dma_start(bet[:, k:k + 1], beta[k * P:(k + 1) * P].rearrange("(p c) -> p c", c=1)).then_inc(s_small, 16)
                sp.dma_start(wr_t[:, k, :], Wr[k * P:(k + 1) * P, :]).then_inc(s_small, 16)
                sp.dma_start(w_t[:, k, :], gnn_W[k * P:(k + 1) * P, :]).then_inc(s_small, 16)
            for e in range(NE):
                for m in range(KH):
                    sp.dma_start(b1_t[:, e * KH + m:e * KH + m + 1],
                                 b1[e, m * P:(m + 1) * P].rearrange("(p c) -> p c", c=1)).then_inc(s_small, 16)
            for q in range(SB):
                sp.dma_start(b2_t[32 * q:32 * q + NE, q, :], b2[:, :]).then_inc(s_small, 16)
            sp.dma_start(br_t[:, :], br.rearrange("(a n) -> a n", a=1)).then_inc(s_small, 16)
            sp.dma_start(bias_f[:, :], gnn_bias.rearrange("(a n) -> a n", a=1)).then_inc(s_small, 16)
            for n in range(2 * NE):
                e, second = n // 2, n % 2
                if n >= NWS:
                    sp.wait_ge(s_wlo, n - NWS + 1)
                w = (W2[e].rearrange("(k p) n -> p k n", p=P) if second
                     else W1[e].rearrange("(k p) n -> p k n", p=P))
                dst_w = wstage[:, n % NWS, :].rearrange("p (k n) -> p k n", k=KH if second else KD)
                sp.dma_start(dst_w, w).then_inc(s_wload[n % NWS], 16)
            sp.wait_ge(s_zt, 1)
            for i in range(NCLR):
                w_ = zeros_rec.shape[1]
                sp.dma_start(clear_v[:, i * w_:(i + 1) * w_], zeros_rec[:, :]).then_inc(s_clear, 16)

            sp.dma_start(xt[0][PAD:P, :], x[0:P - PAD, :]).then_inc(s_xload, 16)
            reached(sp, s_ln, 1)
            sp.dma_start(xt[0][:, :], x[P - PAD:2 * P - PAD, :]).then_inc(s_xload, 16)
            reached(sp, s_hhl, 1)
            sp.dma_start(h_table[0:P - PAD, :], hrow_hl[PAD:P, :]).then_inc(s_hst, 16)
            with sp.Fori(2, NT) as b:
                reached(sp, s_ln, b)
                sp.dma_start(xt[0][:, :], x[ds(b * P - PAD, P), :]).then_inc(s_xload, 16)
                reached(sp, s_hhl, b)
                sp.dma_start(h_table[ds((b - 1) * P - PAD, P), :], hrow_hl[:, :]).then_inc(s_hst, 16)
            reached(sp, s_hhl, NT)
            sp.dma_start(h_table[(NT - 1) * P - PAD:N, :], hrow_hl[:, :]).then_inc(s_hst, 16)

            sp.wait_ge(s_tables, 1)
            blocks = sp.value_load(blocks_n[0:1, 0:1], min_val=-(-NT // RQ), max_val=-(-MAXQ // RQ))
            for g in range(NG):
                sp.wait_ge(s_scat[g], 16 * GC * TURNS)
            list_v = edge_list.rearrange("(b p r) c -> b p (r c)", p=P, r=BLK)

            def load_block(b):
                sp.dma_start(rec[:, ds((b % RECB) * BLK * 4, BLK * 4)],
                             list_v[ds(b, 1), :, :].rearrange("b p n -> p (b n)")).then_inc(s_recl, 16)

            def relay(b):
                reached(sp, s_tgt, (b - 2) * RG)
                load_block(b + 1)
                reached(sp, s_recl, 16 * (b + 2))
                for k in range(SLOTS):
                    reached(sp, s_gat[k], 16 * (b + 1), gate=False)
                    if k % QC == QC - 1:
                        sp.sem_inc(s_gath, 1)

            load_block(0)
            sp.wait_ge(s_recl, 16)
            for b in range(3):
                relay(b)
            with sp.Fori(3, blocks) as b:
                relay(b)

        @block.gpsimd
        def _(pool):
            nc.gpsimd.memset(ident[:, :], 0.0).then_inc(s_const, 1)
            nc.gpsimd.memset(before_b[:, :], 1.0).then_inc(s_const, 1)
            nc.gpsimd.iota(iota_i[:, :], pattern=[[1, P]], base=0, channel_multiplier=0).then_inc(s_const, 1)
            pool.wait_ge(s_const, 3)
            nc.gpsimd.affine_select(out=ident[:, :], in_=ident[:, :], compare_op=ALU.not_equal, fill=1.0,
                                    base=0, pattern=[[-1, P]], channel_multiplier=1).then_inc(s_const, 1)
            nc.gpsimd.affine_select(out=before_b[:, :], in_=before_b[:, :], compare_op=ALU.is_gt, fill=0.0,
                                    base=0, pattern=[[1, P]], channel_multiplier=-1).then_inc(s_const, 1)
            for n in range(2 * NE):
                e, second = n // 2, n % 2
                hi = (w2h if second else w1h)[:, e, :, :].rearrange("p k n -> p (k n)")
                lo = (w2l if second else w1l)[:, e, :, :].rearrange("p k n -> p (k n)")
                slot = wstage[:, n % NWS, :]
                pool.wait_ge(s_whi, n + 1)
                nc.gpsimd.tensor_scalar(slot, slot, WSCALE, None, ALU.mult).then_inc(s_wtmp, 1)
                pool.wait_ge(s_wtmp, n + 1)
                nc.gpsimd.tensor_tensor(lo, slot, hi, ALU.subtract).then_inc(s_wlo, 1)

            pool.wait_ge(s_clear, 16 * NCLR)

            def scatter(i):
                for g in range(NG):
                    reached(pool, s_row, (i * NG + g) + 1)
                    reached(pool, s_rec, (i * NG + g) + 1)
                    for c in range(GC):
                        pool.indirect_dma_start(
                            out=edge_list[:, :], out_offset=bass.IndirectOffsetOnAxis(ap=list_row[g][:, c:c + 1], axis=0),
                            in_=record[g][:, c, :], in_offset=None).then_inc(s_scat[g], 16)

            scatter(0)
            with pool.Fori(1, TURNS) as i:
                scatter(i)

            blocks = pool.value_load(blocks_n[0:1, 0:1], min_val=-(-NT // RQ), max_val=-(-MAXQ // RQ))
            pool.wait_ge(s_hst, 16 * NT)

            def ids(b, j):
                reached(pool, s_gath, (b - 1) * RQ + (j + 1) * SEG // QC)
                first = ((b % RECB) * BLK + j * SEG) * 4
                nc.gpsimd.tensor_copy(row_id[j][:, :], rec[:, ds(first, SEG * 4)].rearrange(
                    "p (r c) -> p r c", c=4)[:, :, 0]).then_inc(s_ids, 1)

            def gather(b):
                reached(pool, s_recl, 16 * (b + 1))
                ids(b, 0)
                for j in range(BLK // SEG):
                    if j + 1 < BLK // SEG:
                        ids(b, j + 1)
                    reached(pool, s_ids, b * (BLK // SEG) + j + 1)
                    for k in range(j * SEG, (j + 1) * SEG):
                        if k % QC == 0:
                            reached(pool, s_summed, b * RQ + k // QC + 1)
                        pool.indirect_dma_start(
                            out=stage[:, k * 2 * D:(k + 1) * 2 * D], out_offset=None, in_=h_table[:, :],
                            in_offset=bass.IndirectOffsetOnAxis(ap=row_id[j][:, k % SEG:k % SEG + 1], axis=0),
                        ).then_inc(s_gat[k], 16)

            gather(0)
            with pool.Fori(1, blocks) as b:
                gather(b)

        @block.scalar
        def _(act):
            for n in range(2 * NE):
                e, second = n // 2, n % 2
                hi = (w2h if second else w1h)[:, e, :, :].rearrange("p k n -> p (k n)")
                act.wait_ge(s_wload[n % NWS], 16 * (n // NWS + 1))
                nc.scalar.activation(hi, wstage[:, n % NWS, :], ACT.Copy, scale=WSCALE).then_inc(s_whi, 1)
            act.wait_ge(s_small, 16 * NSMALL)
            nc.scalar.activation(bias_hl[0:1, 0:D], bias_f[:, :], ACT.Copy).then_inc(s_bias, 1)

            act.wait_ge(s_tables, 1)

            def turn(i, tile):
                for g in range(NG):
                    reached(act, s_scat[g], 16 * GC * i)
                    col = ds(i * TC + g * GC, GC)
                    nc.scalar.activation(record[g][:, :, 0], dst_i[:, col], ACT.Copy)
                    nc.scalar.activation(record[g][:, :, 1], row_in_tile[:, col], ACT.Copy)
                    nc.scalar.activation(record[g][:, :, 2], w_high[:, col], ACT.Copy)
                    nc.scalar.activation(record[g][:, :, 3], wgt[:, col], ACT.Copy).then_inc(s_rec, 1)
                    if tile and g == 1:
                        reached(act, s_lntr, i + 1)
                        reached(act, s_hmm, i)
                        nc.scalar.activation(lnt[:, :, :].rearrange("p k n -> p (k n)"), psT[:, 0:KD * P],
                                             ACT.Copy).then_inc(s_lnt, 1)
                    if tile and g == 3:
                        reached(act, s_hmm, i + 1)
                        reached(act, s_hst, 16 * i)
                        reached(act, s_hhl, i)
                        nc.scalar.activation(hrow_hl[:, 0:D], psM[:, 0:D], ACT.Copy)
                        nc.scalar.activation(hrow[:, :], psM[:, 0:D], ACT.Copy).then_inc(s_hrow, 1)

            turn(0, True)
            with act.Fori(1, NT) as i:
                turn(i, True)
            with act.Fori(NT, TURNS) as i:
                turn(i, False)

            act.wait_ge(s_tables, 1)

            def load_x(b, par):
                reached(act, s_x1, b - 1)
                act.dma_start(xt[par][:, :], x[ds(b * P - PAD, P), :]).then_inc(s_xl[par], 16)

            def transposed(b, par, spar, q):
                reached(act, s_tr, b + 1)
                reached(act, s_lgm, b - 1)
                reached(act, s_xTl, b - 1)
                for k in range(KD):
                    nc.scalar.activation(xT[par][:, k, :], psT[:, k * P:(k + 1) * P], ACT.Identity,
                                         scale=gam[:, k:k + 1], bias=bet[:, k:k + 1])
                for k in range(KD):
                    last = nc.scalar.activation(xTh[:, spar, k, q * P:(q + 1) * P], psT[:, k * P:(k + 1) * P],
                                                ACT.Identity, scale=gam[:, k:k + 1], bias=bet[:, k:k + 1])
                last.then_inc(s_xTh, 1)

            def gelus(f, e):
                n0 = f * NHC + e * KH
                reached(act, s_y, f * YPS + SB + (e - 2) * SB + SB if e >= 2 else
                        (f - 1) * YPS + SB + (NE - 2 + e) * SB + SB)
                for m in range(KH):
                    reached(act, s_w1, n0 + m + 1)
                    reached(act, s_hl, n0 + m - 3)
                    nc.scalar.activation(h32[:, m, :], psH[m % 2][:, :], ACT.Gelu,
                                         scale=1.0 / WSCALE, bias=b1_t[:, e * KH + m:e * KH + m + 1])
                    nc.scalar.activation(hh[:, e % 2, m, :], psH[m % 2][:, :], ACT.Gelu,
                                         scale=1.0 / WSCALE,
                                         bias=b1_t[:, e * KH + m:e * KH + m + 1]).then_inc(s_hh, 1)

            def exps(s):
                reached(act, s_diff, s + 1)
                nc.scalar.activation(ex[:, :], diff[:, :], ACT.Exp).then_inc(s_exp, 1)

            def weights_T(f):
                reached(act, s_wtr, f + 1)
                nc.scalar.activation(wT[:, :], psM[:, P:2 * P], ACT.Copy).then_inc(s_wT, 1)

            def step(s, q, f, spar, b, more):
                if b is not None:
                    if more:
                        load_x(b + 1, (q + 1) % 2)
                if f is not None:
                    gelus(f, 2 * q)
                    if q == 0:
                        weights_T(f)
                if b is not None:
                    transposed(b, q % 2, spar, q)
                if f is not None:
                    gelus(f, 2 * q + 1)
                if b is not None and q == (SB - 1):
                    exps(s)

            def store(f, fpar):
                reached(act, s_yadd, (f + 1) * YPS)
                if isinstance(f, int) and f == 0:
                    act.dma_start(out[0:P - PAD, :], acc[PAD:P, 0, 0, :]).then_inc(s_ost, 16)
                    act.dma_start(out[P - PAD:2 * P - PAD, :], acc[:, 0, 1, :]).then_inc(s_ost, 16)
                else:
                    r = (2 + (f - 1) * SB) * P - PAD
                    act.dma_start(out[ds(r, SB * P), :].rearrange("(q p) d -> p q d", p=P),
                                  acc[:, fpar, :, :]).then_inc(s_ost, 16)

            act.wait_ge(s_hrow, NT)
            act.dma_start(xt[0][PAD:P, :], x[0:P - PAD, :]).then_inc(s_xl[0], 16)
            act.dma_start(xt[1][:, :], x[P - PAD:2 * P - PAD, :]).then_inc(s_xl[1], 16)
            transposed(0, 0, 0, 0)
            load_x(2, 0)
            transposed(1, 1, 0, 1)
            exps(0)

            def pair(j, last):
                for h in range(2):
                    s, f = 2 * j + 1 + h, 2 * j + h
                    for q in range(SB):
                        b = 2 + (2 * j + h) * SB + q
                        more = not (last and h == 1 and q == SB - 1)
                        step(s, q, f, 1 - h, b, more)
                    store(f, h)

            pair(0, False)
            with act.Fori(1, NSB // 2 - 1) as j:
                pair(j, False)
            pair(NSB // 2 - 1, True)
            for q in range(SB):
                step(None, q, NSB, None, None, False)
            store(NSB, 0)
            act.wait_ge(s_ost, 16 * (NSB + 2))

        @block.vector
        def _(dve):
            nc.vector.memset(src_i[:, COLS:CH], N).then_inc(s_pad, 1)
            nc.vector.memset(dst_i[:, COLS:CH], 0).then_inc(s_pad, 1)
            nc.vector.memset(wgt[:, COLS:CH], 0.0).then_inc(s_pad, 1)
            nc.vector.memset(b2_t[:, :, :].rearrange("p q d -> p (q d)"), 0.0).then_inc(s_b2z, 1)
            nc.vector.memset(zeros_rec[:, :], 0.0)
            nc.vector.memset(xt[0][:, :], 0.0)
            for g in range(NG):
                last = nc.vector.memset(record[g][:, :, :].rearrange("p c r -> p (c r)"), 0.0)
            last.then_inc(s_zt, 1)
            nc.vector.memset(ones_b[:, :], 1.0)
            nc.vector.memset(ones_f[:, :], 1.0)
            nc.vector.memset(zero_h[:, :], 0.0)
            nc.vector.memset(one_h[:, :], 1.0)
            nc.vector.memset(start_f[:, 0:1], 0.0)
            nc.vector.memset(acc[:, 0, :, :].rearrange("p q d -> p (q d)"), 0.0)
            nc.vector.memset(xTh[:, 0, :, :].rearrange("p k n -> p (k n)"), 0.0)
            nc.vector.memset(xTl[:, 0, :, :].rearrange("p k n -> p (k n)"), 0.0)
            nc.vector.memset(mx[:, :, :].rearrange("p q n -> p (q n)"), 0.0)
            nc.vector.memset(ix[:, :, :].rearrange("p q n -> p (q n)"), 0)
            nc.vector.memset(wfull[:, :, :].rearrange("p q n -> p (q n)"), 0.0)
            dve.wait_ge(s_const, 3)
            nc.vector.tensor_copy(iota_h[:, :], iota_i[:, :])
            for q in range(SB):
                nc.vector.tensor_copy(iota8[:, q, :], iota_i[:, 0:NE])
            nc.vector.tensor_copy(iota_b[:, :], iota_i[:, 0:NB]).then_inc(s_constv, 1)
            dve.wait_ge(s_constv, 1)

            own = [0]

            def then(ins):
                own[0] += 1
                ins.then_inc(s_prep, 1)
                dve.wait_ge(s_prep, own[0])

            dve.wait_ge(s_edges, 16 * 6)
            then(nc.vector.tensor_scalar(src_i[:, :], src_i[:, :], PAD, None, ALU.add))
            row_bits, bucket_bits = row_in_tile[:, :].bitcast(i32), bucket[:, :].bitcast(i32)
            then(nc.vector.tensor_scalar(row_bits, src_i[:, :], P - 1, None, ALU.bitwise_and))
            then(nc.vector.tensor_copy(row_in_tile[:, :], row_bits))
            then(nc.vector.tensor_scalar(bucket_bits, src_i[:, :], 7, None, ALU.logical_shift_right))
            then(nc.vector.tensor_copy(bucket[:, :], bucket_bits))
            then(nc.vector.tensor_copy(w_high[:, :], wgt[:, :]))
            then(nc.vector.tensor_tensor(wgt[:, :], wgt[:, :], w_high[:, :], ALU.subtract))
            dve.wait_ge(s_bias, 1)
            nc.vector.tensor_tensor(bias_hl[0:1, D:2 * D], bias_f[:, :], bias_hl[0:1, 0:D],
                                    ALU.subtract).then_inc(s_bias, 1)
            b2_all = b2_t[:, :, :].rearrange("p q d -> p (q d)")
            nc.vector.tensor_scalar(b2_all, b2_all, WSCALE, None, ALU.mult).then_inc(s_bias, 1)

            def build(i, g, used):
                reached(dve, used, (i - 1) * NG + g + 1, gate=False)
                for c in range(GC):
                    last = nc.vector.tensor_scalar(onehot[:, g, c, :], iota_b[:, :],
                                                   bucket[:, ds(i * TC + g * GC + c, 1)], None, ALU.is_equal)
                last.then_inc(s_oh, 1)

            for g in range(NG):
                build(0, g, s_ohused)
            with dve.Fori(1, TURNS) as i:
                for g in range(NG):
                    build(i, g, s_ohused)

            dve.wait_ge(s_counted, 1)
            then(nc.vector.tensor_reduce(cnt_f[:, :], ps_count[:, 0:GC * NB].rearrange("p (c b) -> p b c", c=GC),
                                         AX.X, ALU.add))
            then(nc.vector.tensor_scalar(cnt_i[:, :], cnt_f[:, :], float(QROWS - 1), None, ALU.add))
            then(nc.vector.tensor_scalar(nch_i[:, :], cnt_i[:, :], 9, None, ALU.logical_shift_right))
            then(nc.vector.tensor_scalar(nch_f[:, :], nch_i[:, :], 1.0, None, ALU.max))
            then(nc.vector.tensor_tensor_scan(start_f[:, 1:NB + 1], ones_f[:, 0:NB], nch_f[:, :], 0.0,
                                              ALU.mult, ALU.add))
            then(nc.vector.tensor_copy(start_i[:, :], start_f[:, :]))
            then(nc.vector.tensor_scalar(run_row[0:1, 0, :], start_f[0:1, 0:NB], float(QROWS), None, ALU.mult))
            then(nc.vector.tensor_scalar(blocks_i[:, :], start_f[:, NT:NT + 1], float(RQ - 1), None, ALU.add))
            then(nc.vector.tensor_scalar(blocks_n[:, :], blocks_i[:, :], 3, None, ALU.logical_shift_right))
            then(nc.vector.tensor_scalar(some_i[:, :], start_f[:, :], float(GQ - 1), None, ALU.add))
            then(nc.vector.tensor_scalar(gstart_i[:, :], some_i[:, :], 1, None, ALU.logical_shift_right))
            then(nc.vector.tensor_scalar(some_i[:, :], start_f[:, :], float(RQ), None, ALU.add))
            then(nc.vector.tensor_scalar(some_i[:, :], some_i[:, :], 1, None, ALU.logical_shift_right))
            then(nc.vector.tensor_tensor(gahead_i[:, :], some_i[:, 0:NB], gstart_i[:, 1:NB + 1], ALU.min))
            dve.sem_inc(s_tables, 1)

            def normalise(out_ap, in_ap, s, base, twice=False):
                nc.vector.bn_stats(stats[:, :], in_ap).then_inc(s, 1)
                reached(dve, s, base + 1)
                nc.vector.bn_aggr(mv[:, :], stats[:, :]).then_inc(s, 1)
                reached(dve, s, base + 2, gate=False)
                if twice:
                    nc.vector.tensor_scalar(ve[:, :], mv[:, 1:2], 1.0 + EPS, EPS * EPS, ALU.mult, ALU.add).then_inc(s, 1)
                else:
                    nc.vector.tensor_scalar(ve[:, :], mv[:, 1:2], EPS, None, ALU.add).then_inc(s, 1)
                reached(dve, s, base + 3, gate=False)
                nc.vector.tensor_scalar(rs[:, :].bitcast(i32), ve[:, :].bitcast(i32), -0.5, float(0x5F3759DF),
                                        ALU.mult, ALU.add).then_inc(s, 1)
                nc.vector.tensor_scalar(vh[:, :], ve[:, :], -0.5, None, ALU.mult).then_inc(s, 1)
                for k in range(3):
                    reached(dve, s, base + 5 + 2 * k, gate=False)
                    nc.vector.scalar_tensor_tensor(rq[:, :], rs[:, :], rs[:, 0:1], vh[:, :], ALU.mult,
                                                   ALU.mult).then_inc(s, 1)
                    reached(dve, s, base + 6 + 2 * k, gate=False)
                    nc.vector.scalar_tensor_tensor(rs[:, :], rq[:, :], 1.5, rs[:, :], ALU.add,
                                                   ALU.mult).then_inc(s, 1)
                reached(dve, s, base + OWN, gate=False)
                return nc.vector.tensor_scalar(out_ap, in_ap, mv[:, 0:1], rs[:, 0:1], ALU.subtract, ALU.mult)

            def select(i, g):
                reached(dve, s_read, i * NG + g, gate=False)
                reached(dve, s_ranks, i * NG + g + 1, gate=False)
                nc.vector.tensor_copy(run_row[0:1, 0, :],
                                      ps_run[g % 2][0:1, GC * NB:(GC + 1) * NB]).then_inc(s_run, 1)
                for c in range(GC):
                    last = nc.vector.scalar_tensor_tensor(
                        chosen[:, c, :], ps_run[g % 2][:, c * NB:(c + 1) * NB], 1.0, onehot[:, g, c, :], ALU.mult, ALU.mult,
                        accum_out=pos_f[:, g * GC + c:g * GC + c + 1])
                last.then_inc(s_read, 1)

            def split_row(n):
                reached(dve, s_hrow, n + 1, gate=False)
                nc.vector.tensor_tensor(hrow_hl[:, D:2 * D], hrow[:, :], hrow_hl[:, 0:D],
                                        ALU.subtract).then_inc(s_hhl, 1)

            def turn(i, tile):
                build(i, 0, s_ranks)
                for g in range(NG):
                    if g + 1 < NG:
                        build(i, g + 1, s_ranks)
                    select(i, g)
                    if tile and g == 2 and not isinstance(i, int):
                        split_row(i - 1)
                    if tile and g == 0:
                        reached(dve, s_xload, 16 * (i + 1))
                        reached(dve, s_lntr, i)
                        normalise(zb[0][:, :], xt[0][:, :], s_own, OWN * i).then_inc(s_ln, 1)
                reached(dve, s_read, (i + 1) * NG, gate=False)
                nc.vector.tensor_copy(pos_i[:, :], pos_f[:, :]).then_inc(s_pos, 1)
                reached(dve, s_pos, 5 * i + 1, gate=False)
                nc.vector.tensor_scalar(pos_a[:, :], pos_i[:, :], -BLK * P, None, ALU.bitwise_and).then_inc(s_pos, 1)
                nc.vector.tensor_scalar(pos_b[:, :], pos_i[:, :], P - 1, 5, ALU.bitwise_and,
                                        ALU.logical_shift_left).then_inc(s_pos, 1)
                nc.vector.tensor_scalar(pos_c[:, :], pos_i[:, :], 7, BLK - 1, ALU.logical_shift_right,
                                        ALU.bitwise_and).then_inc(s_pos, 1)
                reached(dve, s_pos, 5 * i + 4, gate=False)
                nc.vector.tensor_tensor(pos_b[:, :], pos_b[:, :], pos_c[:, :], ALU.bitwise_or).then_inc(s_pos, 1)
                reached(dve, s_pos, 5 * i + 5, gate=False)
                for g in range(NG):
                    reached(dve, s_scat[g], 16 * GC * i, gate=False)
                    nc.vector.tensor_tensor(list_row[g][:, :], pos_a[:, g * GC:(g + 1) * GC],
                                            pos_b[:, g * GC:(g + 1) * GC], ALU.bitwise_or).then_inc(s_row, 1)

            turn(0, True)
            with dve.Fori(1, NT) as i:
                turn(i, True)
            split_row(NT - 1)
            with dve.Fori(NT, TURNS) as i:
                turn(i, False)

            def target_rows(g):
                reached(dve, s_gath, GQ * (g + 1), gate=False)
                reached(dve, s_summed, GQ * (g + 1), gate=False)
                at = (g % RG) * (GQ * QC * 2 * P)
                field = (g % (RECB * RG)) * (GQ * QC * 4)
                for c in range(GQ * QC):
                    for part in range(2):
                        last = nc.vector.tensor_scalar(
                            target[:, ds(at + (2 * c + part) * P, P)], iota_h[:, :],
                            rec[:, ds(field + 4 * c + 1, 1)], rec[:, ds(field + 4 * c + 2 + part, 1)],
                            ALU.is_equal, ALU.mult)
                last.then_inc(s_tgt, 1)

            def table(t, b, biggest):
                return dve.value_load(t[0:1, ds(b, 1)], min_val=0, max_val=biggest)

            def ahead(b, k):
                first, end = table(gstart_i, b, MAXQ), table(gahead_i, b, MAXQ)
                with dve.If(first + k < end):
                    if k < 2:
                        target_rows(first + k)
                    else:
                        with dve.Fori(first + k, end) as g:
                            target_rows(g)

            def rest(b):
                first, end = table(gahead_i, b, MAXQ), table(gstart_i, b + 1, MAXQ)
                with dve.If(first < end):
                    with dve.Fori(first, end) as g:
                        target_rows(g)

            def epilogue(b, par, spar, q, loads, s):
                rows = acc[:, spar, q, :]
                reached(dve, s_agg, b + 1, gate=False)
                reached(dve, s_xl[par], 16 * loads, gate=False)
                if not isinstance(s, int) or s > 1:
                    reached(dve, s_ost, 16 * s, gate=False)
                nc.vector.tensor_tensor(rows, xt[par][:, :], psA[:, 0:D], ALU.add).then_inc(s_own3, 1)
                reached(dve, s_own3, OWN3 * b + 1, gate=False)
                nc.vector.tensor_tensor(rows, rows, psA[:, D:2 * D], ALU.add).then_inc(s_x1, 1)
                reached(dve, s_x1, b + 1, gate=False)
                reached(dve, s_tr, b - 1, gate=False)
                normalise(zb[par][:, :], rows, s_own3, OWN3 * b + 1, twice=True).then_inc(s_z, 1)

            def x_low(b, par, spar, q):
                reached(dve, s_xTh, b + 1, gate=False)
                nc.vector.tensor_tensor(xTl[:, spar, :, q * P:(q + 1) * P], xT[par][:, :, :],
                                        xTh[:, spar, :, q * P:(q + 1) * P], ALU.subtract).then_inc(s_xTl, 1)

            def top2(b, q):
                reached(dve, s_lgm, b + 1, gate=False)
                nc.vector.tensor_copy(lg[:, :], psM[:, 0:NE]).then_inc(s_lgc, 1)
                reached(dve, s_lgc, b + 1)
                nc.vector.max(mx[:, q, :], lg[:, :]).then_inc(s_top, 1)
                reached(dve, s_top, 2 * b + 1)
                nc.vector.max_index(ix[:, q, :], mx[:, q, :], lg[:, :]).then_inc(s_top, 1)

            def finalise(s):
                base = 8 * s
                reached(dve, s_top, 2 * (SB * s + 2), gate=False)
                nc.vector.tensor_tensor(diff[:, :], mx[:, :, 1], mx[:, :, 0], ALU.subtract).then_inc(s_diff, 1)
                nc.vector.tensor_copy(ixf[:, :, :], ix[:, :, 0:2]).then_inc(s_fin, 1)
                reached(dve, s_exp, s + 1, gate=False)
                nc.vector.tensor_scalar(den[:, :], ex[:, :], 1.0, WSCALE, ALU.add, ALU.mult).then_inc(s_fin, 1)
                reached(dve, s_fin, base + 2, gate=False)
                nc.vector.reciprocal(tw[:, :, 0], den[:, :]).then_inc(s_fin, 1)
                reached(dve, s_fin, base + 3, gate=False)
                nc.vector.tensor_tensor(tw[:, :, 1], ex[:, :], tw[:, :, 0], ALU.mult).then_inc(s_fin, 1)
                for k, eq in enumerate((eq0, eq1)):
                    nc.vector.tensor_tensor(eq[:, :, :], iota8[:, :, :], ixf[:, :, k:k + 1].to_broadcast([P, SB, NE]),
                                            ALU.is_equal).then_inc(s_fin, 1)
                reached(dve, s_fin, base + 6, gate=False)
                for k, eq in enumerate((eq0, eq1)):
                    nc.vector.tensor_tensor(eq[:, :, :], eq[:, :, :], tw[:, :, k:k + 1].to_broadcast([P, SB, NE]),
                                            ALU.mult).then_inc(s_fin, 1)
                reached(dve, s_fin, base + 8, gate=False)
                reached(dve, s_wtr, s, gate=False)
                nc.vector.tensor_tensor(wfull[:, :, 0:NE], eq0[:, :, :], eq1[:, :, :], ALU.add).then_inc(s_wf, 1)

            def h_low(f, e):
                for m in range(KH):
                    reached(dve, s_hh, f * NHC + e * KH + m + 1, gate=False)
                    nc.vector.tensor_tensor(hl[:, e % 2, m, :], h32[:, m, :], hh[:, e % 2, m, :],
                                            ALU.subtract).then_inc(s_hl, 1)

            def add_b2(f, fpar):
                reached(dve, s_wf, f + 1, gate=False)
                for q in range(SB):
                    reached(dve, s_y, f * YPS + q + 1, gate=False)
                    nc.vector.tensor_tensor(acc[:, fpar, q, :], acc[:, fpar, q, :], psY[q % 3][:, 0:D],
                                            ALU.add).then_inc(s_yadd, 1)

            def add_expert(f, fpar, e):
                for q in range(SB):
                    y = f * YPS + SB + e * SB + q
                    reached(dve, s_y, y + 1, gate=False)
                    reached(dve, s_yadd, y - SB + 1, gate=False)
                    nc.vector.scalar_tensor_tensor(acc[:, fpar, q, :], psY[(SB + e * SB + q) % 3][:, 0:D], wfull[:, q, e:e + 1],
                                                   acc[:, fpar, q, :], ALU.mult, ALU.add).then_inc(s_yadd, 1)

            def step(s, q, f, spar, b, loads, more=True):
                if b is not None:
                    rest(b)
                if more:
                    ahead(b + 1, 0)
                if b is not None:
                    epilogue(b, q % 2, spar, q, loads, s)
                if f is not None:
                    h_low(f, 2 * q)
                    if q == 0:
                        add_b2(f, 1 - spar)
                    else:
                        add_expert(f, 1 - spar, 2 * q - 1)
                if b is not None:
                    x_low(b, q % 2, spar, q)
                if more:
                    ahead(b + 1, 1)
                if f is not None:
                    h_low(f, 2 * q + 1)
                    add_expert(f, 1 - spar, 2 * q)
                if more:
                    ahead(b + 1, 2)
                if b is not None:
                    top2(b, q)
                if f is not None and q == SB - 1:
                    add_expert(f, 1 - spar, 2 * q + 1)
                if b is not None and q == (1 if f is None else SB - 1):
                    finalise(s)

            dve.wait_ge(s_recl, 16)
            dve.wait_ge(s_rec, TURNS * NG)
            for k in range(3):
                ahead(0, k)
            for q in range(2):
                step(0, q, None, 0, q, 1)

            def pair(j, last):
                for h in range(2):
                    for q in range(SB):
                        b = 2 + (2 * j + h) * SB + q
                        step(2 * j + 1 + h, q, 2 * j + h, 1 - h, b, 2 + 4 * j + 2 * h + q // 2,
                             not (last and h == 1 and q == SB - 1))

            pair(0, False)
            with dve.Fori(1, NSB // 2 - 1) as j:
                pair(j, False)
            pair(NSB // 2 - 1, True)
            for q in range(SB):
                step(None, q, NSB, 1, None, None, False)

        @block.tensor
        def _(pe):
            pe.wait_ge(s_constv, 1)
            flat = [onehot[:, g, :, :].rearrange("p c b -> p (c b)") for g in range(NG)]
            NG_B = GC * NB

            nc.tensor.matmul(ps_count[:, 0:NG_B], zero_h[:, 0:P], zero_h[:, 0:NG_B], start=True, stop=False)

            def count(i):
                for g in range(NG):
                    reached(pe, s_oh, i * NG + g + 1)
                    nc.tensor.matmul(ps_count[:, 0:NG_B], ones_b[:, :], flat[g], start=False,
                                     stop=False).then_inc(s_ohused, 1)

            count(0)
            with pe.Fori(1, TURNS) as i:
                count(i)
            nc.tensor.matmul(ps_count[:, 0:NG_B], zero_h[:, 0:P], zero_h[:, 0:NG_B], start=False,
                             stop=True).then_inc(s_counted, 1)

            GROUPS = TURNS * NG
            pe.wait_ge(s_tables, 1)

            def turn(i, tile):
                for g in range(NG):
                    group = i * NG + g
                    reached(pe, s_oh, GROUPS + group + 1)
                    reached(pe, s_run, group)
                    reached(pe, s_read, group - 1)
                    ps = ps_run[g % 2]
                    copies = ps[:, 0:(GC + 1) * NB].rearrange("p (c b) -> p c b", b=NB)
                    nc.tensor.matmul(copies, ones_f[0:1, 0:P], run_row[0:1, :, :].to_broadcast([1, GC + 1, NB]),
                                     start=True, stop=False)
                    for c in range(GC):
                        n = GC - c
                        nc.tensor.matmul(copies[:, c + 1:, :], ones_b[:, :],
                                         onehot[:, g, c:c + 1, :].to_broadcast([P, n, NB]), start=False, stop=False)
                    nc.tensor.matmul(ps[:, 0:NG_B], before_b[:, :], flat[g], start=False,
                                     stop=True).then_inc(s_ranks, 1)
                    if tile and g == 1:
                        reached(pe, s_ln, i + 1)
                        reached(pe, s_lnt, i)
                        for k in range(KD):
                            last = nc.tensor.transpose(psT[:, k * P:(k + 1) * P], zb[0][:, k * P:(k + 1) * P], ident[:, :])
                        last.then_inc(s_lntr, 1)
                    if tile and g == 2:
                        reached(pe, s_lnt, i + 1)
                        reached(pe, s_hrow, i)
                        for k in range(KD):
                            last = nc.tensor.matmul(psM[:, 0:D], lnt[:, k, :], w_t[:, k, :], start=(k == 0),
                                                    stop=(k == KD - 1))
                        last.then_inc(s_hmm, 1)

            pe.wait_ge(s_small, 16 * NSMALL)
            turn(0, True)
            with pe.Fori(1, NT) as i:
                turn(i, True)
            with pe.Fori(NT, TURNS) as i:
                turn(i, False)

            pe.wait_ge(s_bias, 3)
            pe.wait_ge(s_wlo, 2 * NE)
            pe.wait_ge(s_hrow, NT)
            pe.wait_ge(s_read, TURNS * NG)
            pe.sem_inc(s_summed, RQ)

            def chunks(b):
                reached(pe, s_x1, b)
                nc.tensor.matmul(psA[:, :], one_h[:, :], bias_hl[:, :], start=True, stop=False)
                lo_t = pe.value_load(start_i[0:1, ds(b, 1)], min_val=0, max_val=MAXQ)
                hi_t = pe.value_load(start_i[0:1, ds(b + 1, 1)], min_val=1, max_val=MAXQ)
                with pe.Fori(lo_t, hi_t) as t:
                    reached(pe, s_tgt, t // GQ + 1)
                    at, rows = (t % RQ) * (QC * 2 * P), (t % RQ) * (QC * 2 * D)
                    for c in range(QC):
                        nc.tensor.matmul(psA[:, :], target[:, ds(at + 2 * c * P, P)],
                                         stage[:, ds(rows + 2 * c * D, 2 * D)], start=False, stop=False)
                        last = nc.tensor.matmul(psA[:, 0:D], target[:, ds(at + (2 * c + 1) * P, P)],
                                                stage[:, ds(rows + 2 * c * D, D)], start=False, stop=False)
                    last.then_inc(s_summed, 1)
                nc.tensor.matmul(psA[:, :], zero_h[:, 0:P], zero_h[:, :], start=False,
                                 stop=True).then_inc(s_agg, 1)

            def transposes(b, par):
                reached(pe, s_z, b + 1)
                reached(pe, s_xTh, b)
                for k in range(KD):
                    last = nc.tensor.transpose(psT[:, k * P:(k + 1) * P], zb[par][:, k * P:(k + 1) * P], ident[:, :])
                last.then_inc(s_tr, 1)

            def logits(b, par):
                reached(pe, s_xTh, b + 1)
                reached(pe, s_lgc, b)
                nc.tensor.matmul(psM[:, 0:NE], ones_f[0:1, 0:P], br_t[:, :], start=True, stop=False)
                for k in range(KD):
                    last = nc.tensor.matmul(psM[:, 0:NE], xT[par][:, k, :], wr_t[:, k, :], start=False,
                                            stop=(k == KD - 1))
                last.then_inc(s_lgm, 1)

            def hidden(f, fpar, e):
                for m in range(KH):
                    reached(pe, s_hh, f * NHC + e * KH + m - 1)
                    col = slice(m * P, (m + 1) * P)
                    for k in range(KD):
                        wh, wl = w1h[:, e, k, col], w1l[:, e, k, col]
                        xh, xl = xTh[:, fpar, k, :], xTl[:, fpar, k, :]
                        for n, (a, c) in enumerate(((wh, xh), (wh, xl), (wl, xh))):
                            last = nc.tensor.matmul(psH[m % 2][:, :], a, c, start=(k == 0 and n == 0),
                                                    stop=(k == KD - 1 and n == 2))
                    last.then_inc(s_w1, 1)

            def expert(f, e):
                reached(pe, s_hl, f * NHC + (e + 1) * KH)
                for q in range(SB):
                    reached(pe, s_yadd, f * YPS + SB + e * SB + q - 2)
                    rows = slice(q * P, (q + 1) * P)
                    for m in range(KH):
                        ah, al = hh[:, e % 2, m, rows], hl[:, e % 2, m, rows]
                        for n, (a, c) in enumerate(((ah, w2h), (ah, w2l), (al, w2h))):
                            last = nc.tensor.matmul(psY[(SB + e * SB + q) % 3][:, 0:D], a, c[:, e, m, :], start=(m == 0 and n == 0),
                                                    stop=(m == KH - 1 and n == 2))
                    last.then_inc(s_y, 1)

            def b2_terms(f):
                reached(pe, s_wf, f + 1)
                reached(pe, s_wT, f)
                nc.tensor.transpose(psM[:, P:2 * P], wfull[:, :, :].rearrange("p q e -> p (q e)"),
                                    ident[:, :]).then_inc(s_wtr, 1)
                reached(pe, s_wT, f + 1)
                for q in range(SB):
                    reached(pe, s_yadd, f * YPS + q - 2)
                    nc.tensor.matmul(psY[q % 3][:, 0:D], wT[:, :], b2_t[:, q, :], start=True,
                                     stop=True).then_inc(s_y, 1)

            def step(q, f, spar, b):
                if b is not None:
                    chunks(b)
                if f is not None:
                    if q == 0:
                        reached(pe, s_xTl, SB * f + 2)
                    hidden(f, 1 - spar, 2 * q)
                    if q == 0:
                        b2_terms(f)
                    else:
                        expert(f, 2 * q - 1)
                if b is not None:
                    transposes(b, q % 2)
                if f is not None:
                    hidden(f, 1 - spar, 2 * q + 1)
                    expert(f, 2 * q)
                if b is not None:
                    logits(b, q % 2)
                if f is not None and q == SB - 1:
                    expert(f, 2 * q + 1)

            for q in range(2):
                step(q, None, 0, q)

            def pair(j):
                for h in range(2):
                    for q in range(SB):
                        step(q, 2 * j + h, 1 - h, 2 + (2 * j + h) * SB + q)

            pair(0)
            with pe.Fori(1, NSB // 2) as j:
                pair(j)
            for q in range(SB):
                step(q, NSB, 1, None)


_INS = ["x", "src", "dst", "edge_weight", "L0_gnn_W", "L0_gnn_bias", "L0_ffn_gamma", "L0_ffn_beta", "L0_ffn_Wr",
        "L0_ffn_br", "L0_ffn_W1", "L0_ffn_b1", "L0_ffn_W2", "L0_ffn_b2"]


def kernel(**inputs):
    import numpy as _np
    import concourse.bacc as _bacc
    from concourse import mybir as _mybir
    from concourse.bass_utils import run_bass_kernel_spmd as _run

    nc = _bacc.Bacc("TRN2", target_bir_lowering=False, num_devices=1)
    arrays, args = {}, []
    for name in _INS:
        a = _np.ascontiguousarray(inputs[name])
        arrays[f"in_{name}_dram"] = a
        args.append(nc.dram_tensor(f"in_{name}_dram", a.shape, _mybir.dt.from_np(a.dtype), kind="ExternalInput").ap())
    f32 = _mybir.dt.float32
    rows, cols = inputs["x"].shape
    h_table = nc.dram_tensor("h_table", (rows, 2 * cols), _mybir.dt.float16).ap()
    edge_list = nc.dram_tensor("edge_list", (66 * 4096, 4), f32).ap()
    out = nc.dram_tensor("out_0_dram", (rows, cols), f32, kind="ExternalOutput").ap()
    gnn_moe_layer_kernel(nc, *args, h_table, edge_list, out)
    r = _run(nc, [arrays], core_ids=[0])
    return r.results[0]["out_0_dram"]
```

```python
import concourse.bass as bass
from concourse import mybir
from contextlib import ExitStack


def gnn_moe_layer_kernel(
    nc: bass.Bass,
    x: bass.AP,
    src: bass.AP,
    dst: bass.AP,
    edge_weight: bass.AP,
    gnn_W: bass.AP,
    gnn_bias: bass.AP,
    gamma: bass.AP,
    beta: bass.AP,
    Wr: bass.AP,
    br: bass.AP,
    W1: bass.AP,
    b1: bass.AP,
    W2: bass.AP,
    b2: bass.AP,
    h_table: bass.AP,
    edge_list: bass.AP,
    out: bass.AP,
):
    fp32 = mybir.dt.float32
    fp16 = mybir.dt.float16
    bf16 = mybir.dt.bfloat16
    i32 = mybir.dt.int32
    u32 = mybir.dt.uint32
    ALU = mybir.AluOpType
    ACT = mybir.ActivationFunctionType
    ds = bass.ds

    P = 128
    N, D = x.shape
    E = src.shape[0]
    NE, _, HID = W1.shape
    KD = D // P
    KH = HID // P
    NT = -(-N // P)
    PAD = NT * P - N
    EPS = 1e-5
    WSCALE = 64.0

    GC = 4
    NG = 4
    TC = GC * NG
    COLS = E // P
    LEFT = E - COLS * P
    TURNS = -(-(COLS + (LEFT > 0)) // TC)
    CH = TURNS * TC
    NB = NT + 2
    assert NB * GC <= 512 and NT < TURNS - 2 and NT % 2 == TURNS % 2 == 0 and PAD > 0

    BLK = 32
    SEG = 8
    RECB = 4
    QC = 4
    QROWS = QC * P
    MAXQ = E // QROWS + 1 + NT
    SLOTS = 32
    RQ = SLOTS // QC
    GQ = 2
    RG = RQ // GQ
    assert BLK == SLOTS and -(-MAXQ // RQ) + 1 <= edge_list.shape[0] // (BLK * P)
    assert QROWS == 512 and RQ == 8 and GQ == 2

    SB = 4
    NSB = (NT - 2) // SB
    assert NT == 2 + SB * NSB and NSB % 2 == 0
    NHC = NE * KH
    YPS = SB * NE + SB
    assert YPS % 3 == 0

    ctx = ExitStack()
    with ctx:
        ctx.enter_context(nc.allow_non_contiguous_dma(reason="small constants, one element per row"))

        def sb(name, shape, dt):
            return ctx.enter_context(nc.sbuf_tensor(name, shape, dt))

        def sem(name):
            return ctx.enter_context(nc.semaphore(name))

        chosen = sb("chosen", [P, GC, NB], fp32)
        w_high = sb("w_high", [P, CH], fp16)
        pos_f = sb("pos_f", [P, TC], fp32)
        pos_i = sb("pos_i", [P, TC], i32)
        pos_a = sb("pos_a", [P, TC], i32)
        pos_b = sb("pos_b", [P, TC], i32)
        pos_c = sb("pos_c", [P, TC], i32)
        list_row = [[sb(f"list_row{t}_{g}", [P, GC], i32) for g in range(NG)] for t in range(2)]
        record = [[sb(f"record{t}_{g}", [P, GC, 4], fp32) for g in range(NG)] for t in range(2)]
        bucket_h = sb("bucket_h", [P, CH], fp16)
        bucket_no = sb("bucket_no", [P, NB], fp32)
        cnt_part = sb("cnt_part", [P, NB], fp32)

        cnt_f = sb("cnt_f", [P, NB], fp32)
        cnt_i = sb("cnt_i", [P, NB], i32)
        nch_i = sb("nch_i", [P, NB], i32)
        nch_f = sb("nch_f", [P, NB], fp32)
        ones_f = sb("ones_f", [P, P], fp32)
        start_f = sb("start_f", [P, NB + 1], fp32)
        start_i = sb("start_i", [P, NB + 1], i32)
        some_i = sb("some_i", [P, NB + 1], i32)
        gstart_i = sb("gstart_i", [P, NB + 1], i32)
        gahead_i = sb("gahead_i", [P, NB], i32)
        run_row = sb("run_row", [1, 1, NB], fp32)
        blocks_i = sb("blocks_i", [P, 1], i32)
        blocks_n = sb("blocks_n", [P, 1], i32)

        ident = sb("ident", [P, P], fp32)
        iota_i = sb("iota_i", [P, P], i32)
        iota_h = sb("iota_h", [P, P], fp16)
        iota_b = sb("iota_b", [P, NB], bf16)
        ones_b = sb("ones_b", [P, P], bf16)
        before_b = sb("before_b", [P, P], bf16)
        zero_h = sb("zero_h", [1, 512], fp16)
        one_h = sb("one_h", [1, P], fp16)
        bias_f = sb("bias_f", [1, D], fp32)
        bias_hl = sb("bias_hl", [1, 2 * D], fp16)
        gam = sb("gam", [P, KD], fp32)
        bet = sb("bet", [P, KD], fp32)
        b1_t = sb("b1_t", [P, NHC], fp32)
        wr_t = sb("wr_t", [P, KD, NE], fp32)
        br_t = sb("br_t", [1, NE], fp32)
        b2_t = sb("b2_t", [P, SB, D], fp32)
        w_t = sb("w_t", [P, KD, D], fp32)
        w1h = sb("w1h", [P, NE, KD, HID], fp16)
        w1l = sb("w1l", [P, NE, KD, HID], fp16)
        w2h = sb("w2h", [P, NE, KH, D], fp16)
        w2l = sb("w2l", [P, NE, KH, D], fp16)

        xt = [sb(f"xt{i}", [P, D], fp32) for i in range(2)]
        stats = sb("stats", [P, 6], fp32)
        mv = sb("mv", [P, 2], fp32)
        ve = sb("ve", [P, 1], fp32)
        vh = sb("vh", [P, 1], fp32)
        rs = sb("rs", [P, 1], fp32)
        rq = sb("rq", [P, 1], fp32)
        zb = [sb(f"zb{i}", [P, D], fp32) for i in range(2)]
        lnt = sb("lnt", [P, KD, P], fp32)
        hrow = sb("hrow", [P, D], fp32)
        hrow_hl = sb("hrow_hl", [P, 2 * D], fp16)

        rec = sb("rec", [P, RECB * BLK * 4], fp32)
        row_id = [sb(f"row_id{j}", [P, SEG], i32) for j in range(BLK // SEG)]
        stage = sb("stage", [P, SLOTS * 2 * D], fp16)
        room = sb("room", [P, 4 * CH], fp32)
        acc = sb("acc", [P, 2, SB, D], fp32)
        xT = [sb(f"xT{i}", [P, KD, P], fp32) for i in range(2)]
        xTh = sb("xTh", [P, 2, KD, SB * P], fp16)
        xTl = sb("xTl", [P, 2, KD, SB * P], fp16)
        h32 = sb("h32", [P, 4, 512], fp32)
        hh = sb("hh", [P, 2, KH, 512], fp16)
        hl = sb("hl", [P, 2, KH, 512], fp16)
        lg = sb("lg", [P, NE], fp32)
        mx = sb("mx", [P, SB, 8], fp32)
        ix = sb("ix", [P, SB, 8], u32)
        ixf = sb("ixf", [P, SB, 2], fp32)
        diff = sb("diff", [P, SB], fp32)
        ex = sb("ex", [P, SB], fp32)
        unused = sb("unused", [P, 1], fp32)
        den = sb("den", [P, SB], fp32)
        tw = sb("tw", [P, SB, 2], fp32)
        iota8 = sb("iota8", [P, SB, NE], fp32)
        eq0 = sb("eq0", [P, SB, NE], fp32)
        eq1 = sb("eq1", [P, SB, NE], fp32)
        wfull = sb("wfull", [P, SB, 32], fp32)
        wT = sb("wT", [P, P], fp32)

        target = room[:, 0:SLOTS * P].bitcast(fp16)
        dst_i = room[:, 0:CH].bitcast(i32)
        wgt = room[:, CH:2 * CH]
        bucket = room[:, 2 * CH:3 * CH]
        row_in_tile = room[:, 3 * CH:4 * CH]
        src_i = h32[:, :, :].rearrange("p a b -> p (a b)")[:, 0:CH].bitcast(i32)
        zeros_rec = hh[:, :, :, :].rearrange("p a b c -> p (a b c)").bitcast(fp32)[:, 0:1056]
        onehot = hl[:, :, :, :].rearrange("p a b c -> p (a b c)").bitcast(bf16)[:, 0:TC * NB].rearrange(
            "p (g c b) -> p g c b", g=NG, c=GC)
        compared = hl[:, :, :, :].rearrange("p a b c -> p (a b c)")[:, 0:2 * CH].rearrange(
            "p (n c) -> p n c", n=2)
        wstage = stage[:, :].bitcast(fp32).rearrange("p (a b) -> p a b", b=KD * HID)
        NWS = wstage.shape[1]

        bank = [ctx.enter_context(nc.psum_tensor(f"bank{i}", [P, 512], fp32)) for i in range(8)]
        psA, psH, psY, psT, psM = bank[0], bank[2:4], [bank[4], bank[5], bank[1]], bank[6], bank[7]
        ps_count, ps_run = bank[2], bank[0:2]

        s_pad = sem("s_pad")
        s_edges = sem("s_edges")
        s_small = sem("s_small")
        s_b2z = sem("s_b2z")
        s_const = sem("s_const")
        s_constv = sem("s_constv")
        s_wload = [sem(f"s_wload{i}") for i in range(NWS)]
        s_whi = sem("s_whi")
        s_wlo = sem("s_wlo")
        s_bias = sem("s_bias")
        s_prep = sem("s_prep")
        s_oh = sem("s_oh")
        s_cntp = sem("s_cntp")
        s_counted = sem("s_counted")
        s_tables = sem("s_tables")
        s_run = sem("s_run")
        s_ranks = sem("s_ranks")
        s_read = sem("s_read")
        s_pos = sem("s_pos")
        s_row = sem("s_row")
        s_rec = sem("s_rec")
        s_scat = [[sem(f"s_scat{t}_{g}") for g in range(NG)] for t in range(2)]
        s_clear = sem("s_clear")
        s_zt = sem("s_zt")
        s_xload = sem("s_xload")
        s_ln = sem("s_ln")
        s_own = sem("s_own")
        s_lntr = sem("s_lntr")
        s_lnt = sem("s_lnt")
        s_hmm = sem("s_hmm")
        s_hrow = sem("s_hrow")
        s_hhl = sem("s_hhl")
        s_hst = sem("s_hst")
        s_gate = sem("s_gate")

        s_recl = sem("s_recl")
        s_ids = sem("s_ids")
        s_gat = [sem(f"s_gat{k}") for k in range(SLOTS)]
        s_gath = sem("s_gath")
        s_tgt = sem("s_tgt")
        s_summed = sem("s_summed")
        s_agg = sem("s_agg")
        s_xl = [sem("s_xl0"), sem("s_xl1")]
        s_x1 = sem("s_x1")
        s_z = sem("s_z")
        s_own3 = sem("s_own3")
        s_tr = sem("s_tr")
        s_xTh = sem("s_xTh")
        s_xTl = sem("s_xTl")
        s_lgm = sem("s_lgm")
        s_lgc = sem("s_lgc")
        s_top = sem("s_top")
        s_diff = sem("s_diff")
        s_exp = sem("s_exp")
        s_table = sem("s_table")
        s_fin = sem("s_fin")
        s_wf = sem("s_wf")
        s_wtr = sem("s_wtr")
        s_wT = sem("s_wT")
        s_w1 = sem("s_w1")
        s_hh = sem("s_hh")
        s_hl = sem("s_hl")
        s_y = sem("s_y")
        s_yadd = sem("s_yadd")
        s_ost = sem("s_ost")

        def reached(eng, s, value, gate=True):
            if isinstance(value, int):
                if value > 0:
                    eng.wait_ge(s, value)
                return
            eng.wait_ge(s, value)
            if gate:
                eng.sem_inc(s_gate, 1)

        clear_v = edge_list.rearrange("(p a) c -> p (a c)", p=P)
        NCLR = clear_v.shape[1] // zeros_rec.shape[1]
        assert NCLR * zeros_rec.shape[1] == clear_v.shape[1]

        NSMALL = 4 * KD + NHC + SB + 2
        OWN = 11
        OWN3 = OWN + 1

        block = ctx.enter_context(nc.Block())

        @block.sync
        def _(sp):
            sp.wait_ge(s_pad, 3)
            for t, a in ((src_i, src), (dst_i, dst), (wgt, edge_weight)):
                sp.dma_start(t[:, 0:COLS], a[0:COLS * P].rearrange("(p c) -> p c", p=P)).then_inc(s_edges, 16)
                sp.dma_start(t[0:LEFT, COLS:COLS + 1],
                             a[COLS * P:E].rearrange("(p c) -> p c", c=1)).then_inc(s_edges, 16)
            sp.wait_ge(s_zt, 1)
            for i in range(NCLR):
                w_ = zeros_rec.shape[1]
                sp.dma_start(clear_v[:, i * w_:(i + 1) * w_], zeros_rec[:, :]).then_inc(s_clear, 16)
            sp.wait_ge(s_b2z, 1)
            for k in range(KD):
                sp.dma_start(gam[:, k:k + 1], gamma[k * P:(k + 1) * P].rearrange("(p c) -> p c", c=1)).then_inc(s_small, 16)
                sp.dma_start(bet[:, k:k + 1], beta[k * P:(k + 1) * P].rearrange("(p c) -> p c", c=1)).then_inc(s_small, 16)
                sp.dma_start(wr_t[:, k, :], Wr[k * P:(k + 1) * P, :]).then_inc(s_small, 16)
                sp.dma_start(w_t[:, k, :], gnn_W[k * P:(k + 1) * P, :]).then_inc(s_small, 16)
            for e in range(NE):
                for m in range(KH):
                    sp.dma_start(b1_t[:, e * KH + m:e * KH + m + 1],
                                 b1[e, m * P:(m + 1) * P].rearrange("(p c) -> p c", c=1)).then_inc(s_small, 16)
            for q in range(SB):
                sp.dma_start(b2_t[32 * q:32 * q + NE, q, :], b2[:, :]).then_inc(s_small, 16)
            sp.dma_start(br_t[:, :], br.rearrange("(a n) -> a n", a=1)).then_inc(s_small, 16)
            sp.dma_start(bias_f[:, :], gnn_bias.rearrange("(a n) -> a n", a=1)).then_inc(s_small, 16)
            for n in range(2 * NE):
                e, second = n // 2, n % 2
                if n >= NWS:
                    sp.wait_ge(s_wlo, n - NWS + 1)
                w = (W2[e].rearrange("(k p) n -> p k n", p=P) if second
                     else W1[e].rearrange("(k p) n -> p k n", p=P))
                dst_w = wstage[:, n % NWS, :].rearrange("p (k n) -> p k n", k=KH if second else KD)
                sp.dma_start(dst_w, w).then_inc(s_wload[n % NWS], 16)
            sp.dma_start(xt[0][PAD:P, :], x[0:P - PAD, :]).then_inc(s_xload, 16)
            reached(sp, s_ln, 1)
            sp.dma_start(xt[0][:, :], x[P - PAD:2 * P - PAD, :]).then_inc(s_xload, 16)
            reached(sp, s_hhl, 1)
            sp.dma_start(h_table[0:P - PAD, :], hrow_hl[PAD:P, :]).then_inc(s_hst, 16)
            with sp.Fori(2, NT) as b:
                reached(sp, s_ln, b)
                sp.dma_start(xt[0][:, :], x[ds(b * P - PAD, P), :]).then_inc(s_xload, 16)
                reached(sp, s_hhl, b)
                sp.dma_start(h_table[ds((b - 1) * P - PAD, P), :], hrow_hl[:, :]).then_inc(s_hst, 16)
            reached(sp, s_hhl, NT)
            sp.dma_start(h_table[(NT - 1) * P - PAD:N, :], hrow_hl[:, :]).then_inc(s_hst, 16)

            sp.wait_ge(s_tables, 1)
            blocks = sp.value_load(blocks_n[0:1, 0:1], min_val=-(-NT // RQ), max_val=-(-MAXQ // RQ))
            for t in range(2):
                for g in range(NG):
                    sp.wait_ge(s_scat[t][g], 16 * GC * (TURNS // 2))
            list_v = edge_list.rearrange("(b p r) c -> b p (r c)", p=P, r=BLK)

            def load_block(b):
                sp.dma_start(rec[:, ds((b % RECB) * BLK * 4, BLK * 4)],
                             list_v[ds(b, 1), :, :].rearrange("b p n -> p (b n)")).then_inc(s_recl, 16)

            def relay(b):
                reached(sp, s_tgt, (b - 2) * RG)
                load_block(b + 1)
                reached(sp, s_recl, 16 * (b + 2))
                for k in range(SLOTS):
                    reached(sp, s_gat[k], 16 * (b + 1), gate=False)
                    if k % QC == QC - 1:
                        sp.sem_inc(s_gath, 1)

            load_block(0)
            sp.wait_ge(s_recl, 16)
            for b in range(3):
                relay(b)
            with sp.Fori(3, blocks) as b:
                relay(b)

        @block.gpsimd
        def _(pool):
            nc.gpsimd.memset(ident[:, :], 0.0).then_inc(s_const, 1)
            nc.gpsimd.memset(before_b[:, :], 1.0).then_inc(s_const, 1)
            nc.gpsimd.iota(iota_i[:, :], pattern=[[1, P]], base=0, channel_multiplier=0).then_inc(s_const, 1)
            pool.wait_ge(s_const, 3)
            nc.gpsimd.affine_select(out=ident[:, :], in_=ident[:, :], compare_op=ALU.not_equal, fill=1.0,
                                    base=0, pattern=[[-1, P]], channel_multiplier=1).then_inc(s_const, 1)
            nc.gpsimd.affine_select(out=before_b[:, :], in_=before_b[:, :], compare_op=ALU.is_gt, fill=0.0,
                                    base=0, pattern=[[1, P]], channel_multiplier=-1).then_inc(s_const, 1)
            for n in range(2 * NE):
                e, second = n // 2, n % 2
                hi = (w2h if second else w1h)[:, e, :, :].rearrange("p k n -> p (k n)")
                lo = (w2l if second else w1l)[:, e, :, :].rearrange("p k n -> p (k n)")
                slot = wstage[:, n % NWS, :]
                pool.wait_ge(s_whi, n + 1)
                nc.gpsimd.tensor_tensor(lo, slot, hi, ALU.subtract).then_inc(s_wlo, 1)

            pool.wait_ge(s_clear, 16 * NCLR)

            def scatter(i, par):
                for g in range(NG):
                    reached(pool, s_row, (i * NG + g) + 1)
                    reached(pool, s_rec, (i * NG + g) + 1)
                    for c in range(GC):
                        pool.indirect_dma_start(
                            out=edge_list[:, :],
                            out_offset=bass.IndirectOffsetOnAxis(ap=list_row[par][g][:, c:c + 1], axis=0),
                            in_=record[par][g][:, c, :], in_offset=None).then_inc(s_scat[par][g], 16)

            scatter(0, 0)
            scatter(1, 1)
            with pool.Fori(1, TURNS // 2) as j:
                scatter(2 * j, 0)
                scatter(2 * j + 1, 1)

            blocks = pool.value_load(blocks_n[0:1, 0:1], min_val=-(-NT // RQ), max_val=-(-MAXQ // RQ))
            pool.wait_ge(s_hst, 16 * NT)

            def ids(b, j):
                reached(pool, s_gath, (b - 1) * RQ + (j + 1) * SEG // QC)
                first = ((b % RECB) * BLK + j * SEG) * 4
                nc.gpsimd.tensor_copy(row_id[j][:, :], rec[:, ds(first, SEG * 4)].rearrange(
                    "p (r c) -> p r c", c=4)[:, :, 0]).then_inc(s_ids, 1)

            def gather(b):
                reached(pool, s_recl, 16 * (b + 1))
                ids(b, 0)
                for j in range(BLK // SEG):
                    if j + 1 < BLK // SEG:
                        ids(b, j + 1)
                    reached(pool, s_ids, b * (BLK // SEG) + j + 1)
                    for k in range(j * SEG, (j + 1) * SEG):
                        if k % QC == 0:
                            reached(pool, s_summed, b * RQ + k // QC + 1)
                        pool.indirect_dma_start(
                            out=stage[:, k * 2 * D:(k + 1) * 2 * D], out_offset=None, in_=h_table[:, :],
                            in_offset=bass.IndirectOffsetOnAxis(ap=row_id[j][:, k % SEG:k % SEG + 1], axis=0),
                        ).then_inc(s_gat[k], 16)

            gather(0)
            with pool.Fori(1, blocks) as b:
                gather(b)

        @block.scalar
        def _(act):
            for n in range(2 * NE):
                e, second = n // 2, n % 2
                hi = (w2h if second else w1h)[:, e, :, :].rearrange("p k n -> p (k n)")
                act.wait_ge(s_wload[n % NWS], 16 * (n // NWS + 1))
                nc.scalar.activation(hi, wstage[:, n % NWS, :], ACT.Copy, scale=WSCALE)
                nc.scalar.activation(wstage[:, n % NWS, :], wstage[:, n % NWS, :], ACT.Copy,
                                     scale=WSCALE).then_inc(s_whi, 1)
            act.wait_ge(s_small, 16 * NSMALL)
            nc.scalar.activation(bias_hl[0:1, 0:D], bias_f[:, :], ACT.Copy).then_inc(s_bias, 1)

            act.wait_ge(s_tables, 1)

            def turn(j, par, tile):
                i = 2 * j + par
                for g in range(NG):
                    reached(act, s_scat[par][g], 16 * GC * j)
                    col = ds(i * TC + g * GC, GC)
                    nc.scalar.activation(record[par][g][:, :, 0], dst_i[:, col], ACT.Copy)
                    nc.scalar.activation(record[par][g][:, :, 1], row_in_tile[:, col], ACT.Copy)
                    nc.scalar.activation(record[par][g][:, :, 2], w_high[:, col], ACT.Copy)
                    nc.scalar.activation(record[par][g][:, :, 3], wgt[:, col], ACT.Copy).then_inc(s_rec, 1)
                    if tile and g == 1:
                        reached(act, s_lntr, i + 1)
                        reached(act, s_hmm, i)
                        nc.scalar.activation(lnt[:, :, :].rearrange("p k n -> p (k n)"), psT[:, 0:KD * P],
                                             ACT.Copy).then_inc(s_lnt, 1)
                    if tile and g == 3:
                        reached(act, s_hmm, i + 1)
                        reached(act, s_hst, 16 * i)
                        reached(act, s_hhl, i)
                        nc.scalar.activation(hrow_hl[:, 0:D], psM[:, 0:D], ACT.Copy)
                        nc.scalar.activation(hrow[:, :], psM[:, 0:D], ACT.Copy).then_inc(s_hrow, 1)

            turn(0, 0, True)
            turn(0, 1, True)
            with act.Fori(1, NT // 2) as j:
                turn(j, 0, True)
                turn(j, 1, True)
            with act.Fori(NT // 2, TURNS // 2) as j:
                turn(j, 0, False)
                turn(j, 1, False)

            act.wait_ge(s_tables, 1)

            def load_x(b, par):
                reached(act, s_x1, b - 1)
                act.dma_start(xt[par][:, :], x[ds(b * P - PAD, P), :]).then_inc(s_xl[par], 16)

            def transposed(b, par, spar, q):
                reached(act, s_tr, b + 1)
                reached(act, s_lgm, b - 1)
                reached(act, s_xTl, b - 1)
                for k in range(KD):
                    nc.scalar.activation(xT[par][:, k, :], psT[:, k * P:(k + 1) * P], ACT.Identity,
                                         scale=gam[:, k:k + 1], bias=bet[:, k:k + 1])
                for k in range(KD):
                    last = nc.scalar.activation(xTh[:, spar, k, q * P:(q + 1) * P], psT[:, k * P:(k + 1) * P],
                                                ACT.Identity, scale=gam[:, k:k + 1], bias=bet[:, k:k + 1])
                last.then_inc(s_xTh, 1)

            def gelus(f, e):
                n0 = f * NHC + e * KH
                reached(act, s_y, f * YPS + SB + (e - 2) * SB + SB if e >= 2 else
                        (f - 1) * YPS + SB + (NE - 2 + e) * SB + SB)
                for m in range(KH):
                    reached(act, s_w1, n0 + m + 1)
                    reached(act, s_hl, n0 + m - 3)
                    nc.scalar.activation(h32[:, m, :], psH[m % 2][:, :], ACT.Gelu,
                                         scale=1.0 / WSCALE, bias=b1_t[:, e * KH + m:e * KH + m + 1])
                    nc.scalar.activation(hh[:, e % 2, m, :], psH[m % 2][:, :], ACT.Gelu,
                                         scale=1.0 / WSCALE,
                                         bias=b1_t[:, e * KH + m:e * KH + m + 1]).then_inc(s_hh, 1)

            def exps(s):
                reached(act, s_diff, s + 1)
                nc.scalar.activation(ex[:, :], diff[:, :], ACT.Exp).then_inc(s_exp, 1)
                reached(act, s_table, s)
                nc.scalar.activation(unused[:, :], ones_f[:, 0:1], ACT.Gelu).then_inc(s_table, 1)

            def weights_T(f):
                reached(act, s_wtr, f + 1)
                nc.scalar.activation(wT[:, :], psM[:, P:2 * P], ACT.Copy).then_inc(s_wT, 1)

            def step(s, q, f, spar, b, more):
                if b is not None:
                    if more:
                        load_x(b + 1, (q + 1) % 2)
                if f is not None:
                    if q == 0:
                        weights_T(f)
                    gelus(f, 2 * q)
                if b is not None:
                    transposed(b, q % 2, spar, q)
                if f is not None:
                    gelus(f, 2 * q + 1)
                if b is not None and q == (SB - 1):
                    exps(s)

            def store(f, fpar):
                reached(act, s_yadd, (f + 1) * YPS)
                if isinstance(f, int) and f == 0:
                    act.dma_start(out[0:P - PAD, :], acc[PAD:P, 0, 0, :]).then_inc(s_ost, 16)
                    act.dma_start(out[P - PAD:2 * P - PAD, :], acc[:, 0, 1, :]).then_inc(s_ost, 16)
                else:
                    r = (2 + (f - 1) * SB) * P - PAD
                    act.dma_start(out[ds(r, SB * P), :].rearrange("(q p) d -> p q d", p=P),
                                  acc[:, fpar, :, :]).then_inc(s_ost, 16)

            act.wait_ge(s_hrow, NT)
            act.dma_start(xt[0][PAD:P, :], x[0:P - PAD, :]).then_inc(s_xl[0], 16)
            act.dma_start(xt[1][:, :], x[P - PAD:2 * P - PAD, :]).then_inc(s_xl[1], 16)
            transposed(0, 0, 0, 0)
            load_x(2, 0)
            transposed(1, 1, 0, 1)
            exps(0)

            def pair(j, last):
                for h in range(2):
                    s, f = 2 * j + 1 + h, 2 * j + h
                    for q in range(SB):
                        b = 2 + (2 * j + h) * SB + q
                        more = not (last and h == 1 and q == SB - 1)
                        step(s, q, f, 1 - h, b, more)
                    store(f, h)

            pair(0, False)
            with act.Fori(1, NSB // 2 - 1) as j:
                pair(j, False)
            pair(NSB // 2 - 1, True)
            for q in range(SB):
                step(None, q, NSB, None, None, False)
            store(NSB, 0)
            act.wait_ge(s_ost, 16 * (NSB + 2))

        @block.vector
        def _(dve):
            nc.vector.memset(src_i[:, COLS:CH], N).then_inc(s_pad, 1)
            nc.vector.memset(dst_i[:, COLS:CH], 0).then_inc(s_pad, 1)
            nc.vector.memset(wgt[:, COLS:CH], 0.0).then_inc(s_pad, 1)
            nc.vector.memset(b2_t[:, :, :].rearrange("p q d -> p (q d)"), 0.0).then_inc(s_b2z, 1)
            nc.vector.memset(zeros_rec[:, :], 0.0)
            nc.vector.memset(xt[0][:, :], 0.0)
            for t in range(2):
                for g in range(NG):
                    last = nc.vector.memset(record[t][g][:, :, :].rearrange("p c r -> p (c r)"), 0.0)
            last.then_inc(s_zt, 1)
            nc.vector.memset(cnt_part[:, :], 0.0)
            nc.vector.memset(ones_b[:, :], 1.0)
            nc.vector.memset(ones_f[:, :], 1.0)
            nc.vector.memset(zero_h[:, :], 0.0)
            nc.vector.memset(one_h[:, :], 1.0)
            nc.vector.memset(start_f[:, 0:1], 0.0)
            nc.vector.memset(acc[:, 0, :, :].rearrange("p q d -> p (q d)"), 0.0)
            nc.vector.memset(xTh[:, 0, :, :].rearrange("p k n -> p (k n)"), 0.0)
            nc.vector.memset(xTl[:, 0, :, :].rearrange("p k n -> p (k n)"), 0.0)
            nc.vector.memset(mx[:, :, :].rearrange("p q n -> p (q n)"), 0.0)
            nc.vector.memset(ix[:, :, :].rearrange("p q n -> p (q n)"), 0)
            nc.vector.memset(wfull[:, :, :].rearrange("p q n -> p (q n)"), 0.0)
            dve.wait_ge(s_const, 3)
            nc.vector.tensor_copy(iota_h[:, :], iota_i[:, :])
            for q in range(SB):
                nc.vector.tensor_copy(iota8[:, q, :], iota_i[:, 0:NE])
            nc.vector.tensor_copy(bucket_no[:, :], iota_i[:, 0:NB])
            nc.vector.tensor_copy(iota_b[:, :], iota_i[:, 0:NB]).then_inc(s_constv, 1)
            dve.wait_ge(s_constv, 1)

            own = [0]

            def then(ins):
                own[0] += 1
                ins.then_inc(s_prep, 1)
                dve.wait_ge(s_prep, own[0])

            dve.wait_ge(s_edges, 16 * 6)
            then(nc.vector.tensor_scalar(src_i[:, :], src_i[:, :], PAD, None, ALU.add))
            row_bits, bucket_bits = row_in_tile[:, :].bitcast(i32), bucket[:, :].bitcast(i32)
            then(nc.vector.tensor_scalar(row_bits, src_i[:, :], P - 1, None, ALU.bitwise_and))
            then(nc.vector.tensor_copy(row_in_tile[:, :], row_bits))
            then(nc.vector.tensor_scalar(bucket_bits, src_i[:, :], 7, None, ALU.logical_shift_right))
            then(nc.vector.tensor_copy(bucket[:, :], bucket_bits))
            then(nc.vector.tensor_copy(bucket_h[:, :], bucket[:, :]))

            UNROLL = 14
            assert NT % UNROLL == 0 and UNROLL % 2 == 0

            def count(n):
                for u in range(UNROLL):
                    k = n * UNROLL + u
                    reached(dve, s_cntp, k - 1, gate=False)
                    nc.vector.tensor_scalar(compared[:, u % 2, :], bucket_h[:, :], bucket_no[:, ds(k, 1)], 0.0,
                                            ALU.is_equal, ALU.add,
                                            accum_out=cnt_part[:, ds(k, 1)]).then_inc(s_cntp, 1)

            count(0)
            with dve.Fori(1, NT // UNROLL) as n:
                count(n)

            then(nc.vector.tensor_copy(w_high[:, :], wgt[:, :]))
            then(nc.vector.tensor_tensor(wgt[:, :], wgt[:, :], w_high[:, :], ALU.subtract))
            dve.wait_ge(s_counted, 1)
            then(nc.vector.tensor_copy(cnt_f[:, :], ps_count[:, 0:NB]))
            then(nc.vector.tensor_scalar(cnt_i[:, :], cnt_f[:, :], float(QROWS - 1), None, ALU.add))
            then(nc.vector.tensor_scalar(nch_i[:, :], cnt_i[:, :], 9, None, ALU.logical_shift_right))
            then(nc.vector.tensor_scalar(nch_f[:, :], nch_i[:, :], 1.0, None, ALU.max))
            then(nc.vector.tensor_tensor_scan(start_f[:, 1:NB + 1], ones_f[:, 0:NB], nch_f[:, :], 0.0,
                                              ALU.mult, ALU.add))
            then(nc.vector.tensor_copy(start_i[:, :], start_f[:, :]))
            then(nc.vector.tensor_scalar(run_row[0:1, 0, :], start_f[0:1, 0:NB], float(QROWS), None, ALU.mult))
            then(nc.vector.tensor_scalar(blocks_i[:, :], start_f[:, NT:NT + 1], float(RQ - 1), None, ALU.add))
            then(nc.vector.tensor_scalar(blocks_n[:, :], blocks_i[:, :], 3, None, ALU.logical_shift_right))
            then(nc.vector.tensor_scalar(some_i[:, :], start_f[:, :], float(GQ - 1), None, ALU.add))
            then(nc.vector.tensor_scalar(gstart_i[:, :], some_i[:, :], 1, None, ALU.logical_shift_right))
            then(nc.vector.tensor_scalar(some_i[:, :], start_f[:, :], float(RQ), None, ALU.add))
            then(nc.vector.tensor_scalar(some_i[:, :], some_i[:, :], 1, None, ALU.logical_shift_right))
            then(nc.vector.tensor_tensor(gahead_i[:, :], some_i[:, 0:NB], gstart_i[:, 1:NB + 1], ALU.min))
            dve.sem_inc(s_tables, 1)

            def normalise(out_ap, in_ap, s, base, twice=False):
                nc.vector.bn_stats(stats[:, :], in_ap).then_inc(s, 1)
                reached(dve, s, base + 1)
                nc.vector.bn_aggr(mv[:, :], stats[:, :]).then_inc(s, 1)
                reached(dve, s, base + 2, gate=False)
                if twice:
                    nc.vector.tensor_scalar(ve[:, :], mv[:, 1:2], 1.0 + EPS, EPS * EPS, ALU.mult, ALU.add).then_inc(s, 1)
                else:
                    nc.vector.tensor_scalar(ve[:, :], mv[:, 1:2], EPS, None, ALU.add).then_inc(s, 1)
                reached(dve, s, base + 3, gate=False)
                nc.vector.tensor_scalar(rs[:, :].bitcast(i32), ve[:, :].bitcast(i32), -0.5, float(0x5F3759DF),
                                        ALU.mult, ALU.add).then_inc(s, 1)
                nc.vector.tensor_scalar(vh[:, :], ve[:, :], -0.5, None, ALU.mult).then_inc(s, 1)
                for k in range(3):
                    reached(dve, s, base + 5 + 2 * k, gate=False)
                    nc.vector.scalar_tensor_tensor(rq[:, :], rs[:, :], rs[:, 0:1], vh[:, :], ALU.mult,
                                                   ALU.mult).then_inc(s, 1)
                    reached(dve, s, base + 6 + 2 * k, gate=False)
                    nc.vector.scalar_tensor_tensor(rs[:, :], rq[:, :], 1.5, rs[:, :], ALU.add,
                                                   ALU.mult).then_inc(s, 1)
                reached(dve, s, base + OWN, gate=False)
                return nc.vector.tensor_scalar(out_ap, in_ap, mv[:, 0:1], rs[:, 0:1], ALU.subtract, ALU.mult)

            def build(i, g):
                reached(dve, s_ranks, (i - 1) * NG + g + 1, gate=False)
                for c in range(GC):
                    last = nc.vector.tensor_scalar(onehot[:, g, c, :], iota_b[:, :],
                                                   bucket[:, ds(i * TC + g * GC + c, 1)], None, ALU.is_equal)
                last.then_inc(s_oh, 1)

            def select(i, g):
                reached(dve, s_read, i * NG + g, gate=False)
                reached(dve, s_ranks, i * NG + g + 1, gate=False)
                nc.vector.tensor_copy(run_row[0:1, 0, :],
                                      ps_run[g % 2][0:1, GC * NB:(GC + 1) * NB]).then_inc(s_run, 1)
                for c in range(GC):
                    last = nc.vector.scalar_tensor_tensor(
                        chosen[:, c, :], ps_run[g % 2][:, c * NB:(c + 1) * NB], 1.0, onehot[:, g, c, :], ALU.mult, ALU.mult,
                        accum_out=pos_f[:, g * GC + c:g * GC + c + 1])
                last.then_inc(s_read, 1)

            def split_row(n):
                reached(dve, s_hrow, n + 1, gate=False)
                nc.vector.tensor_tensor(hrow_hl[:, D:2 * D], hrow[:, :], hrow_hl[:, 0:D],
                                        ALU.subtract).then_inc(s_hhl, 1)

            def turn(j, par, tile, last=False):
                i = 2 * j + par
                for g in range(NG):
                    if g + 1 < NG:
                        build(i, g + 1)
                    elif not last:
                        build(i + 1, 0)
                    select(i, g)
                    if tile and g == 2 and not (isinstance(i, int) and i == 0):
                        split_row(i - 1)
                    if tile and g == 0:
                        reached(dve, s_xload, 16 * (i + 1))
                        reached(dve, s_lntr, i)
                        normalise(zb[0][:, :], xt[0][:, :], s_own, OWN * i).then_inc(s_ln, 1)
                reached(dve, s_read, (i + 1) * NG, gate=False)
                nc.vector.tensor_copy(pos_i[:, :], pos_f[:, :]).then_inc(s_pos, 1)
                reached(dve, s_pos, 5 * i + 1, gate=False)
                nc.vector.tensor_scalar(pos_a[:, :], pos_i[:, :], -BLK * P, None, ALU.bitwise_and).then_inc(s_pos, 1)
                nc.vector.tensor_scalar(pos_b[:, :], pos_i[:, :], P - 1, 5, ALU.bitwise_and,
                                        ALU.logical_shift_left).then_inc(s_pos, 1)
                nc.vector.tensor_scalar(pos_c[:, :], pos_i[:, :], 7, BLK - 1, ALU.logical_shift_right,
                                        ALU.bitwise_and).then_inc(s_pos, 1)
                reached(dve, s_pos, 5 * i + 4, gate=False)
                nc.vector.tensor_tensor(pos_b[:, :], pos_b[:, :], pos_c[:, :], ALU.bitwise_or).then_inc(s_pos, 1)
                reached(dve, s_pos, 5 * i + 5, gate=False)
                for g in range(NG):
                    reached(dve, s_scat[par][g], 16 * GC * j, gate=False)
                    nc.vector.tensor_tensor(list_row[par][g][:, :], pos_a[:, g * GC:(g + 1) * GC],
                                            pos_b[:, g * GC:(g + 1) * GC], ALU.bitwise_or).then_inc(s_row, 1)

            build(0, 0)
            turn(0, 0, True)
            turn(0, 1, True)
            with dve.Fori(1, NT // 2) as j:
                turn(j, 0, True)
                turn(j, 1, True)
            split_row(NT - 1)
            with dve.Fori(NT // 2, TURNS // 2 - 1) as j:
                turn(j, 0, False)
                turn(j, 1, False)
            turn(TURNS // 2 - 1, 0, False)
            turn(TURNS // 2 - 1, 1, False, last=True)

            def target_rows(g):
                reached(dve, s_gath, GQ * (g + 1), gate=False)
                reached(dve, s_summed, GQ * (g + 1), gate=False)
                at = (g % RG) * (GQ * QC * 2 * P)
                field = (g % (RECB * RG)) * (GQ * QC * 4)
                for c in range(GQ * QC):
                    for part in range(2):
                        last = nc.vector.tensor_scalar(
                            target[:, ds(at + (2 * c + part) * P, P)], iota_h[:, :],
                            rec[:, ds(field + 4 * c + 1, 1)], rec[:, ds(field + 4 * c + 2 + part, 1)],
                            ALU.is_equal, ALU.mult)
                last.then_inc(s_tgt, 1)

            def table(t, b, biggest):
                return dve.value_load(t[0:1, ds(b, 1)], min_val=0, max_val=biggest)

            def ahead(k, first, end):
                with dve.If(end > first + k):
                    if k < 2:
                        target_rows(first + k)
                    else:
                        with dve.Fori(first + k, end) as g:
                            target_rows(g)

            def rest(first, end):
                with dve.If(first < end):
                    with dve.Fori(first, end) as g:
                        target_rows(g)

            def epilogue(b, par, spar, q, loads, s):
                rows = acc[:, spar, q, :]
                reached(dve, s_agg, b + 1, gate=False)
                reached(dve, s_xl[par], 16 * loads, gate=False)
                if not isinstance(s, int) or s > 1:
                    reached(dve, s_ost, 16 * s, gate=False)
                nc.vector.tensor_tensor(rows, xt[par][:, :], psA[:, 0:D], ALU.add).then_inc(s_own3, 1)
                reached(dve, s_own3, OWN3 * b + 1, gate=False)
                nc.vector.tensor_tensor(rows, rows, psA[:, D:2 * D], ALU.add).then_inc(s_x1, 1)
                reached(dve, s_x1, b + 1, gate=False)
                reached(dve, s_tr, b - 1, gate=False)
                normalise(zb[par][:, :], rows, s_own3, OWN3 * b + 1, twice=True).then_inc(s_z, 1)

            def x_low(b, par, spar, q):
                reached(dve, s_xTh, b + 1, gate=False)
                nc.vector.tensor_tensor(xTl[:, spar, :, q * P:(q + 1) * P], xT[par][:, :, :],
                                        xTh[:, spar, :, q * P:(q + 1) * P], ALU.subtract).then_inc(s_xTl, 1)

            def top2(b, q):
                reached(dve, s_lgm, b + 1, gate=False)
                nc.vector.tensor_copy(lg[:, :], psM[:, 0:NE]).then_inc(s_lgc, 1)
                reached(dve, s_lgc, b + 1)
                nc.vector.max(mx[:, q, :], lg[:, :]).then_inc(s_top, 1)
                reached(dve, s_top, 2 * b + 1)
                nc.vector.max_index(ix[:, q, :], mx[:, q, :], lg[:, :]).then_inc(s_top, 1)

            def differences(s):
                reached(dve, s_top, 2 * (SB * s + 2), gate=False)
                nc.vector.tensor_tensor(diff[:, :], mx[:, :, 1], mx[:, :, 0], ALU.subtract).then_inc(s_diff, 1)
                nc.vector.tensor_copy(ixf[:, :, :], ix[:, :, 0:2]).then_inc(s_fin, 1)
                reached(dve, s_fin, 8 * s + 1, gate=False)
                for k, eq in enumerate((eq0, eq1)):
                    nc.vector.tensor_tensor(eq[:, :, :], iota8[:, :, :], ixf[:, :, k:k + 1].to_broadcast([P, SB, NE]),
                                            ALU.is_equal).then_inc(s_fin, 1)

            def finalise(s):
                base = 8 * s
                reached(dve, s_exp, s + 1, gate=False)
                nc.vector.tensor_scalar(den[:, :], ex[:, :], 1.0, WSCALE, ALU.add, ALU.mult).then_inc(s_fin, 1)
                reached(dve, s_fin, base + 4, gate=False)
                nc.vector.reciprocal(tw[:, :, 0], den[:, :]).then_inc(s_fin, 1)
                reached(dve, s_fin, base + 5, gate=False)
                nc.vector.tensor_tensor(tw[:, :, 1], ex[:, :], tw[:, :, 0], ALU.mult).then_inc(s_fin, 1)
                reached(dve, s_fin, base + 6, gate=False)
                for k, eq in enumerate((eq0, eq1)):
                    nc.vector.tensor_tensor(eq[:, :, :], eq[:, :, :], tw[:, :, k:k + 1].to_broadcast([P, SB, NE]),
                                            ALU.mult).then_inc(s_fin, 1)
                reached(dve, s_fin, base + 8, gate=False)
                reached(dve, s_wtr, s, gate=False)
                nc.vector.tensor_tensor(wfull[:, :, 0:NE], eq0[:, :, :], eq1[:, :, :], ALU.add).then_inc(s_wf, 1)

            def h_low(f, e):
                for m in range(KH):
                    reached(dve, s_hh, f * NHC + e * KH + m + 1, gate=False)
                    nc.vector.tensor_tensor(hl[:, e % 2, m, :], h32[:, m, :], hh[:, e % 2, m, :],
                                            ALU.subtract).then_inc(s_hl, 1)

            def add_b2(f, fpar):
                reached(dve, s_wf, f + 1, gate=False)
                for q in range(SB):
                    reached(dve, s_y, f * YPS + q + 1, gate=False)
                    nc.vector.tensor_tensor(acc[:, fpar, q, :], acc[:, fpar, q, :], psY[q % 3][:, 0:D],
                                            ALU.add).then_inc(s_yadd, 1)

            def add_expert(f, fpar, e, tiles=range(SB)):
                for q in tiles:
                    y = f * YPS + SB + e * SB + q
                    reached(dve, s_y, y + 1, gate=False)
                    reached(dve, s_yadd, y - SB + 1, gate=False)
                    nc.vector.scalar_tensor_tensor(acc[:, fpar, q, :], psY[(SB + e * SB + q) % 3][:, 0:D], wfull[:, q, e:e + 1],
                                                   acc[:, fpar, q, :], ALU.mult, ALU.add).then_inc(s_yadd, 1)

            def step(s, q, f, spar, b, loads, more=True):
                if b is not None:
                    made, first = table(gahead_i, b, MAXQ), table(gstart_i, b + 1, MAXQ)
                    rest(made, first)
                if more:
                    end = table(gahead_i, b + 1, MAXQ)
                if b is not None:
                    epilogue(b, q % 2, spar, q, loads, s)
                if f is not None:
                    h_low(f, 2 * q)
                    if q == 0:
                        add_b2(f, 1 - spar)
                    else:
                        add_expert(f, 1 - spar, 2 * q - 1)
                if b is not None:
                    x_low(b, q % 2, spar, q)
                if more:
                    ahead(0, first, end)
                if f is not None:
                    h_low(f, 2 * q + 1)
                    add_expert(f, 1 - spar, 2 * q, range(1))
                if more:
                    ahead(1, first, end)
                if f is not None:
                    add_expert(f, 1 - spar, 2 * q, range(1, SB))
                final = b is not None and q == (1 if f is None else SB - 1)
                if final:
                    top2(b, q)
                    differences(s)
                if f is not None and q == SB - 1:
                    add_expert(f, 1 - spar, 2 * q + 1)
                if more:
                    ahead(2, first, end)
                if final:
                    finalise(s)
                elif b is not None:
                    top2(b, q)

            dve.wait_ge(s_recl, 16)
            dve.wait_ge(s_bias, 1)
            nc.vector.tensor_tensor(bias_hl[0:1, D:2 * D], bias_f[:, :], bias_hl[0:1, 0:D],
                                    ALU.subtract).then_inc(s_bias, 1)
            b2_all = b2_t[:, :, :].rearrange("p q d -> p (q d)")
            nc.vector.tensor_scalar(b2_all, b2_all, WSCALE, None, ALU.mult).then_inc(s_bias, 1)
            dve.wait_ge(s_rec, TURNS * NG)
            end = table(gahead_i, 0, MAXQ)
            for k in range(3):
                ahead(k, 0, end)
            for q in range(2):
                step(0, q, None, 0, q, 1)

            def pair(j, last):
                for h in range(2):
                    for q in range(SB):
                        b = 2 + (2 * j + h) * SB + q
                        step(2 * j + 1 + h, q, 2 * j + h, 1 - h, b, 2 + 4 * j + 2 * h + q // 2,
                             not (last and h == 1 and q == SB - 1))

            pair(0, False)
            with dve.Fori(1, NSB // 2 - 1) as j:
                pair(j, False)
            pair(NSB // 2 - 1, True)
            for q in range(SB):
                step(None, q, NSB, 1, None, None, False)

        @block.tensor
        def _(pe):
            pe.wait_ge(s_constv, 1)
            flat = [onehot[:, g, :, :].rearrange("p c b -> p (c b)") for g in range(NG)]
            NG_B = GC * NB

            pe.wait_ge(s_cntp, NT)
            nc.tensor.matmul(ps_count[:, 0:NB], ones_f[:, :], cnt_part[:, :], start=True,
                             stop=True).then_inc(s_counted, 1)

            pe.wait_ge(s_tables, 1)

            def turn(i, tile):
                for g in range(NG):
                    group = i * NG + g
                    reached(pe, s_oh, group + 1)
                    reached(pe, s_run, group)
                    reached(pe, s_read, group - 1)
                    ps = ps_run[g % 2]
                    copies = ps[:, 0:(GC + 1) * NB].rearrange("p (c b) -> p c b", b=NB)
                    nc.tensor.matmul(copies, ones_f[0:1, 0:P], run_row[0:1, :, :].to_broadcast([1, GC + 1, NB]),
                                     start=True, stop=False)
                    for c in range(GC):
                        n = GC - c
                        nc.tensor.matmul(copies[:, c + 1:, :], ones_b[:, :],
                                         onehot[:, g, c:c + 1, :].to_broadcast([P, n, NB]), start=False, stop=False)
                    nc.tensor.matmul(ps[:, 0:NG_B], before_b[:, :], flat[g], start=False,
                                     stop=True).then_inc(s_ranks, 1)
                    if tile and g == 1:
                        reached(pe, s_ln, i + 1)
                        reached(pe, s_lnt, i)
                        for k in range(KD):
                            last = nc.tensor.transpose(psT[:, k * P:(k + 1) * P], zb[0][:, k * P:(k + 1) * P], ident[:, :])
                        last.then_inc(s_lntr, 1)
                    if tile and g == 2:
                        reached(pe, s_lnt, i + 1)
                        reached(pe, s_hrow, i)
                        for k in range(KD):
                            last = nc.tensor.matmul(psM[:, 0:D], lnt[:, k, :], w_t[:, k, :], start=(k == 0),
                                                    stop=(k == KD - 1))
                        last.then_inc(s_hmm, 1)

            pe.wait_ge(s_small, 16 * NSMALL)
            pe.wait_ge(s_const, 5)
            turn(0, True)
            with pe.Fori(1, NT) as i:
                turn(i, True)
            with pe.Fori(NT, TURNS) as i:
                turn(i, False)

            pe.wait_ge(s_bias, 3)
            pe.wait_ge(s_wlo, 2 * NE)
            pe.wait_ge(s_hrow, NT)
            pe.wait_ge(s_read, TURNS * NG)
            pe.sem_inc(s_summed, RQ)

            def chunks(b):
                reached(pe, s_x1, b)
                nc.tensor.matmul(psA[:, :], one_h[:, :], bias_hl[:, :], start=True, stop=False)
                lo_t = pe.value_load(start_i[0:1, ds(b, 1)], min_val=0, max_val=MAXQ)
                hi_t = pe.value_load(start_i[0:1, ds(b + 1, 1)], min_val=1, max_val=MAXQ)
                with pe.Fori(lo_t, hi_t) as t:
                    reached(pe, s_tgt, t // GQ + 1)
                    at, rows = (t % RQ) * (QC * 2 * P), (t % RQ) * (QC * 2 * D)
                    for c in range(QC):
                        nc.tensor.matmul(psA[:, :], target[:, ds(at + 2 * c * P, P)],
                                         stage[:, ds(rows + 2 * c * D, 2 * D)], start=False, stop=False)
                        last = nc.tensor.matmul(psA[:, 0:D], target[:, ds(at + (2 * c + 1) * P, P)],
                                                stage[:, ds(rows + 2 * c * D, D)], start=False, stop=False)
                    last.then_inc(s_summed, 1)
                nc.tensor.matmul(psA[:, 0:1], zero_h[:, 0:P], zero_h[:, 0:1], start=False,
                                 stop=True).then_inc(s_agg, 1)

            def transposes(b, par):
                reached(pe, s_z, b + 1)
                reached(pe, s_xTh, b)
                for k in range(KD):
                    last = nc.tensor.transpose(psT[:, k * P:(k + 1) * P], zb[par][:, k * P:(k + 1) * P], ident[:, :])
                last.then_inc(s_tr, 1)

            def logits(b, par):
                reached(pe, s_xTh, b + 1)
                reached(pe, s_lgc, b)
                nc.tensor.matmul(psM[:, 0:NE], ones_f[0:1, 0:P], br_t[:, :], start=True, stop=False)
                for k in range(KD):
                    last = nc.tensor.matmul(psM[:, 0:NE], xT[par][:, k, :], wr_t[:, k, :], start=False,
                                            stop=(k == KD - 1))
                last.then_inc(s_lgm, 1)

            def hidden(f, fpar, e):
                for m in range(KH):
                    reached(pe, s_hh, f * NHC + e * KH + m - 1)
                    col = slice(m * P, (m + 1) * P)
                    for k in range(KD):
                        wh, wl = w1h[:, e, k, col], w1l[:, e, k, col]
                        xh, xl = xTh[:, fpar, k, :], xTl[:, fpar, k, :]
                        for n, (a, c) in enumerate(((wh, xh), (wh, xl), (wl, xh))):
                            last = nc.tensor.matmul(psH[m % 2][:, :], a, c, start=(k == 0 and n == 0),
                                                    stop=(k == KD - 1 and n == 2))
                    last.then_inc(s_w1, 1)

            def expert(f, e):
                reached(pe, s_hl, f * NHC + (e + 1) * KH)
                for q in range(SB):
                    reached(pe, s_yadd, f * YPS + SB + e * SB + q - 2)
                    rows = slice(q * P, (q + 1) * P)
                    for m in range(KH):
                        ah, al = hh[:, e % 2, m, rows], hl[:, e % 2, m, rows]
                        for n, (a, c) in enumerate(((ah, w2h), (ah, w2l), (al, w2h))):
                            last = nc.tensor.matmul(psY[(SB + e * SB + q) % 3][:, 0:D], a, c[:, e, m, :], start=(m == 0 and n == 0),
                                                    stop=(m == KH - 1 and n == 2))
                    last.then_inc(s_y, 1)

            def weights_T(f):
                reached(pe, s_wf, f + 1)
                reached(pe, s_wT, f)
                nc.tensor.transpose(psM[:, P:2 * P], wfull[:, :, :].rearrange("p q e -> p (q e)"),
                                    ident[:, :]).then_inc(s_wtr, 1)

            def b2_terms(f):
                reached(pe, s_wT, f + 1)
                for q in range(SB):
                    reached(pe, s_yadd, f * YPS + q - 2)
                    nc.tensor.matmul(psY[q % 3][:, 0:D], wT[:, :], b2_t[:, q, :], start=True,
                                     stop=True).then_inc(s_y, 1)

            def step(q, f, spar, b):
                if b is not None:
                    chunks(b)
                if f is not None:
                    if q == 0:
                        weights_T(f)
                        reached(pe, s_xTl, SB * f + 2)
                    hidden(f, 1 - spar, 2 * q)
                    if q == 0:
                        b2_terms(f)
                    else:
                        expert(f, 2 * q - 1)
                if b is not None:
                    transposes(b, q % 2)
                if f is not None:
                    hidden(f, 1 - spar, 2 * q + 1)
                    expert(f, 2 * q)
                if b is not None:
                    logits(b, q % 2)
                if f is not None and q == SB - 1:
                    expert(f, 2 * q + 1)

            for q in range(2):
                step(q, None, 0, q)

            def pair(j):
                for h in range(2):
                    for q in range(SB):
                        step(q, 2 * j + h, 1 - h, 2 + (2 * j + h) * SB + q)

            pair(0)
            with pe.Fori(1, NSB // 2) as j:
                pair(j)
            for q in range(SB):
                step(q, NSB, 1, None)


_INS = ["x", "src", "dst", "edge_weight", "L0_gnn_W", "L0_gnn_bias", "L0_ffn_gamma", "L0_ffn_beta", "L0_ffn_Wr",
        "L0_ffn_br", "L0_ffn_W1", "L0_ffn_b1", "L0_ffn_W2", "L0_ffn_b2"]


def kernel(**inputs):
    import numpy as _np
    import concourse.bacc as _bacc
    from concourse import mybir as _mybir
    from concourse.bass_utils import run_bass_kernel_spmd as _run

    nc = _bacc.Bacc("TRN2", target_bir_lowering=False, num_devices=1)
    arrays, args = {}, []
    for name in _INS:
        a = _np.ascontiguousarray(inputs[name])
        arrays[f"in_{name}_dram"] = a
        args.append(nc.dram_tensor(f"in_{name}_dram", a.shape, _mybir.dt.from_np(a.dtype), kind="ExternalInput").ap())
    f32 = _mybir.dt.float32
    rows, cols = inputs["x"].shape
    h_table = nc.dram_tensor("h_table", (rows, 2 * cols), _mybir.dt.float16).ap()
    edge_list = nc.dram_tensor("edge_list", (66 * 4096, 4), f32).ap()
    out = nc.dram_tensor("out_0_dram", (rows, cols), f32, kind="ExternalOutput").ap()
    gnn_moe_layer_kernel(nc, *args, h_table, edge_list, out)
    r = _run(nc, [arrays], core_ids=[0])
    return r.results[0]["out_0_dram"]
```
